# Optimizing a Trainium2 kernel written in Bass

```python
import numpy as np
import jax
import jax.numpy as jnp

def _softmax(x, axis=-1):
    return jax.nn.softmax(x, axis=axis)

def _gelu(x):
    return jax.nn.gelu(x, approximate=True)

def _silu(x):
    return jax.nn.silu(x)

def _sigmoid(x):
    return jax.nn.sigmoid(x)

def _layernorm(x, axis=-1, eps=1e-05):
    m = jnp.mean(x, axis=axis, keepdims=True)
    v = jnp.var(x, axis=axis, keepdims=True)
    return (x - m) / jnp.sqrt(v + eps)

def _scatter_add(tgt, idx, src, axis=0):
    return tgt.at[idx].add(src)

def _segment_sum(src, seg, n):
    return jax.ops.segment_sum(src, seg, n)
kernel_name = 'mk_audio_tower_d4_tok_audfeat256_r4_ff6eda'

def setup_inputs(seed: int=0):
    np.random.seed(seed)
    _w = jnp.asarray

    def _rec_inputs():
        import jax
        import jax.numpy as jnp
        _rk = jax.random.key(seed)
        x = -0.000392918 + 0.999932 * jax.random.normal(jax.random.fold_in(_rk, 1), (4, 750, 64), jnp.float32)
        return x
    x = _rec_inputs()

    def _L0_tok_setup():
        import jax, jax.numpy as jnp
        import numpy as np
        from jax import lax
        B, S, CIN, COUT, K = (32, 512, 64, 64, 16)
        key = jax.random.key(seed)
        k1, k2, k3, k4 = jax.random.split(key, 4)
        x = jax.random.normal(k1, (B, S, CIN), dtype=jnp.float32)
        w_real = jax.random.normal(k2, (COUT, CIN, K), dtype=jnp.float32) * 0.1
        w_imag = jax.random.normal(k3, (COUT, CIN, K), dtype=jnp.float32) * 0.1
        phases = jax.random.normal(k4, (K,), dtype=jnp.float32) * 0.1
        return {'x': x, 'w_real': w_real, 'w_imag': w_imag, 'phases': phases}
    _L0_tok_all = _L0_tok_setup()
    _L0_tok_in = {k: v for k, v in _L0_tok_all.items() if k in ('w_real', 'w_imag', 'phases')}
    del _L0_tok_all

    def _L0_attn_setup():
        import jax, jax.numpy as jnp
        import numpy as np
        D_MODEL = 64
        D_STATE = 16
        D_CONV = 4
        EXPAND = 2
        D_INNER = EXPAND * D_MODEL
        DT_RANK = (D_MODEL + 15) // 16
        B_SZ = 4
        SEQ = 1024

        def _mamba_params(key, prefix):
            ks = jax.random.split(key, 6)
            s = 0.02
            return {f'{prefix}_in_w': jax.random.normal(ks[0], (2 * D_INNER, D_MODEL), dtype=jnp.float32) * s, f'{prefix}_conv_w': jax.random.normal(ks[1], (D_INNER, D_CONV), dtype=jnp.float32) * s, f'{prefix}_conv_b': jnp.zeros((D_INNER,), dtype=jnp.float32), f'{prefix}_xproj_w': jax.random.normal(ks[2], (DT_RANK + 2 * D_STATE, D_INNER), dtype=jnp.float32) * s, f'{prefix}_dt_w': jax.random.normal(ks[3], (D_INNER, DT_RANK), dtype=jnp.float32) * s, f'{prefix}_dt_b': jax.random.normal(ks[4], (D_INNER,), dtype=jnp.float32) * s, f'{prefix}_A_log': jnp.log(jnp.tile(jnp.arange(1, D_STATE + 1, dtype=jnp.float32), (D_INNER, 1))), f'{prefix}_D': jnp.ones((D_INNER,), dtype=jnp.float32), f'{prefix}_out_w': jax.random.normal(ks[5], (D_MODEL, D_INNER), dtype=jnp.float32) * s}

        def _mamba(x, in_w, conv_w, conv_b, xproj_w, dt_w, dt_b, A_log, D_param, out_w):
            Bn, L, _ = x.shape
            xz = x @ in_w.T
            xin, z = jnp.split(xz, 2, axis=-1)
            lhs = xin.swapaxes(1, 2)
            rhs = conv_w[:, None, :]
            conv = jax.lax.conv_general_dilated(lhs, rhs, (1,), [(D_CONV - 1, 0)], dimension_numbers=('NCL', 'OIL', 'NCL'), feature_group_count=D_INNER)
            xc = jax.nn.silu(conv.swapaxes(1, 2) + conv_b)
            x_dbl = xc @ xproj_w.T
            dt_low = x_dbl[..., :DT_RANK]
            Bm = x_dbl[..., DT_RANK:DT_RANK + D_STATE]
            Cm = x_dbl[..., DT_RANK + D_STATE:]
            dt = jax.nn.softplus(dt_low @ dt_w.T + dt_b)
            A = -jnp.exp(A_log)

            def step(h, inps):
                dt_t, B_t, C_t, u_t = inps
                dA = jnp.exp(dt_t[:, :, None] * A)
                h = dA * h + dt_t[:, :, None] * B_t[:, None, :] * u_t[:, :, None]
                y = jnp.einsum('bdn,bn->bd', h, C_t)
                return (h, y)
            h0 = jnp.zeros((Bn, D_INNER, D_STATE), dtype=x.dtype)
            xs = (dt.swapaxes(0, 1), Bm.swapaxes(0, 1), Cm.swapaxes(0, 1), xc.swapaxes(0, 1))
            _, ys = jax.lax.scan(step, h0, xs)
            y = ys.swapaxes(0, 1) + D_param * xc
            y = y * jax.nn.silu(z)
            return y @ out_w.T
        key = jax.random.key(seed)
        k1, k2, k3 = jax.random.split(key, 3)
        inp = {'g_data': jax.random.normal(k1, (B_SZ, SEQ, D_MODEL), dtype=jnp.float32)}
        inp.update(_mamba_params(k2, 'f'))
        inp.update(_mamba_params(k3, 'b'))
        return inp
    _L0_attn_all = _L0_attn_setup()
    _L0_attn_in = {k: v for k, v in _L0_attn_all.items() if k in ('f_in_w', 'f_conv_w', 'f_conv_b', 'f_xproj_w', 'f_dt_w', 'f_dt_b', 'f_A_log', 'f_D', 'f_out_w', 'b_in_w', 'b_conv_w', 'b_conv_b', 'b_xproj_w', 'b_dt_w', 'b_dt_b', 'b_A_log', 'b_D', 'b_out_w')}
    del _L0_attn_all

    def _L0_ffn_setup():
        import jax, jax.numpy as jnp
        import numpy as np
        DIM = 64
        HEADS = 8
        NUM_KEYS = 64
        NUM_KV = NUM_KEYS ** 2
        PK_TOPK = 16
        FINAL_TOPK = 16
        DIM_KEY = DIM // 2
        P = 2

        def _pk(x, Wq_pk, pk_keys):
            b, n, _ = x.shape
            q = (x @ Wq_pk).reshape(b, n, P, HEADS, DIM_KEY).transpose(2, 0, 1, 3, 4)
            sim = jnp.einsum('pbnhd,pkhd->pbnhk', q, pk_keys)
            scores, idx = jax.lax.top_k(sim, PK_TOPK)
            idx0 = idx[0]
            idx1 = idx[1] * NUM_KEYS
            index = (idx0[..., :, None] + idx1[..., None, :]).reshape(b, n, HEADS, PK_TOPK * PK_TOPK)
            score = (scores[0][..., :, None] + scores[1][..., None, :]).reshape(b, n, HEADS, PK_TOPK * PK_TOPK)
            final_scores, pk_idx = jax.lax.top_k(score, FINAL_TOPK)
            final_indices = jnp.take_along_axis(index, pk_idx, axis=-1)
            final_scores = jax.nn.softmax(final_scores, axis=-1)
            return (final_scores, final_indices)
        key = jax.random.key(seed)
        ks = jax.random.split(key, 7)
        b, n = (2, 256)
        std = 0.02
        x = jax.random.normal(ks[0], (b, n, DIM), dtype=jnp.float32)
        Wq_pk = jax.random.normal(ks[1], (DIM, P * HEADS * DIM_KEY), dtype=jnp.float32) * std
        pk_keys = jax.random.normal(ks[2], (P, NUM_KEYS, HEADS, DIM_KEY), dtype=jnp.float32) * std
        Wq = jax.random.normal(ks[3], (DIM, HEADS * DIM), dtype=jnp.float32) * std
        keys_table = jax.random.normal(ks[4], (NUM_KV * HEADS, DIM), dtype=jnp.float32) * std
        values_table = jax.random.normal(ks[5], (NUM_KV * HEADS, DIM), dtype=jnp.float32) * std
        Wo = jax.random.normal(ks[6], (DIM * HEADS, DIM), dtype=jnp.float32) * std
        return {'x': x, 'Wq_pk': Wq_pk, 'pk_keys': pk_keys, 'Wq': Wq, 'keys_table': keys_table, 'values_table': values_table, 'Wo': Wo}
    _L0_ffn_all = _L0_ffn_setup()
    _L0_ffn_in = {k: v for k, v in _L0_ffn_all.items() if k in ('Wq_pk', 'pk_keys', 'Wq', 'keys_table', 'values_table', 'Wo')}
    del _L0_ffn_all

    def _L1_attn_setup():
        import jax, jax.numpy as jnp
        import numpy as np
        STATE_DIM = 64
        INPUT_DIM = 64
        OUTPUT_DIM = 64
        BATCH = 16
        SEQ_LEN = 1024
        key = jax.random.key(seed)
        k_in, k_a, k_b, k_c = jax.random.split(key, 4)
        inputs = jax.random.normal(k_in, (BATCH, SEQ_LEN, INPUT_DIM), dtype=jnp.float32)
        A = jnp.clip(jax.random.normal(k_a, (STATE_DIM,), dtype=jnp.float32), -1.0, 1.0)
        B = jax.random.normal(k_b, (INPUT_DIM, STATE_DIM), dtype=jnp.float32) / INPUT_DIM
        C = jax.random.normal(k_c, (STATE_DIM, OUTPUT_DIM), dtype=jnp.float32) / STATE_DIM
        h0 = jnp.zeros((STATE_DIM,), dtype=jnp.float32)
        return {'inputs': inputs, 'A': A, 'B': B, 'C': C, 'h0': h0}
    _L1_attn_all = _L1_attn_setup()
    _L1_attn_in = {k: v for k, v in _L1_attn_all.items() if k in ('A', 'B', 'C', 'h0')}
    del _L1_attn_all

    def _L1_ffn_setup():
        import jax, jax.numpy as jnp
        import numpy as np
        E = 8
        K = 2
        D = 64
        H = 128
        DOUT = 64
        EPS = 1e-05
        key = jax.random.key(seed)
        ks = jax.random.split(key, 9)
        s = 0.02
        return {'x': jax.random.normal(ks[0], (4, 2048, D), jnp.float32), 'gamma': 1.0 + 0.05 * jax.random.normal(ks[1], (D,), jnp.float32), 'beta': 0.05 * jax.random.normal(ks[2], (D,), jnp.float32), 'Wr': 0.01 * jax.random.normal(ks[3], (D, E), jnp.float32), 'br': jnp.zeros((E,), jnp.float32), 'W1': s * jax.random.normal(ks[4], (E, D, H), jnp.float32), 'b1': s * jax.random.normal(ks[5], (E, H), jnp.float32), 'W2': s * jax.random.normal(ks[6], (E, H, DOUT), jnp.float32), 'b2': s * jax.random.normal(ks[7], (E, DOUT), jnp.float32)}
    _L1_ffn_all = _L1_ffn_setup()
    _L1_ffn_in = {k: v for k, v in _L1_ffn_all.items() if k in ('gamma', 'beta', 'Wr', 'br', 'W1', 'b1', 'W2', 'b2')}
    del _L1_ffn_all

    def _L2_attn_setup():
        import jax, jax.numpy as jnp
        import numpy as np
        import math
        B, T, D_MODEL = (1, 512, 64)
        N_Q, N_KV = (16, 1)
        D_HEAD = D_MODEL // N_KV
        QPG = N_Q // N_KV
        ROPE_BASE = 10000.0
        WINDOW = 128
        EPS = 1.1920929e-07
        NEG = -1e+30

        def _rope(x, base=ROPE_BASE):
            t, d = (x.shape[-2], x.shape[-1])
            freqs = base ** (-2.0 * jnp.arange(d // 2, dtype=jnp.float32) / d)
            theta = jnp.arange(t, dtype=jnp.float32)[:, None] * freqs[None, :]
            cos, sin = (jnp.cos(theta), jnp.sin(theta))
            x1, x2 = (x[..., 0::2], x[..., 1::2])
            r1 = x1 * cos - x2 * sin
            r2 = x1 * sin + x2 * cos
            return jnp.stack([r1, r2], axis=-1).reshape(x.shape)

        def _rmsnorm(x, w):
            return x * jax.lax.rsqrt(jnp.mean(x * x, axis=-1, keepdims=True) + EPS) * w
        key = jax.random.key(seed)
        k0, k1, k2, k3 = jax.random.split(key, 4)
        x = jax.random.normal(k0, (B, T, D_MODEL), dtype=jnp.float32)
        wq = jax.random.normal(k1, (QPG * N_KV * D_HEAD, D_MODEL), dtype=jnp.float32) * 0.02
        wkv = jax.random.normal(k2, (2 * D_HEAD * N_KV, D_MODEL), dtype=jnp.float32) * 0.02
        wo = jax.random.normal(k3, (D_MODEL, D_HEAD * N_Q * N_KV), dtype=jnp.float32) * 0.02
        q_norm_w = jnp.ones((D_HEAD,), dtype=jnp.float32)
        k_norm_w = jnp.ones((D_HEAD,), dtype=jnp.float32)
        return {'x': x, 'wq': wq, 'wkv': wkv, 'wo': wo, 'q_norm_w': q_norm_w, 'k_norm_w': k_norm_w}
    _L2_attn_all = _L2_attn_setup()
    _L2_attn_in = {k: v for k, v in _L2_attn_all.items() if k in ('wq', 'wkv', 'wo', 'q_norm_w', 'k_norm_w')}
    del _L2_attn_all

    def _L2_ffn_setup():
        import math
        import jax, jax.numpy as jnp
        import numpy as np
        CAPACITY_FACTOR = 1.25
        key = jax.random.key(seed)
        ks = jax.random.split(key, 5)
        B, L, D, F, E = (8, 2048, 64, 256, 8)
        h = jax.random.normal(ks[0], (B, L, D), dtype=jnp.float32)
        gate_w = jax.random.normal(ks[1], (D, E), dtype=jnp.float32) * 0.02
        gate_b = jnp.zeros((E,), dtype=jnp.float32)
        w1 = jax.random.normal(ks[2], (E, D, F), dtype=jnp.float32) * (1.0 / math.sqrt(D))
        b1 = jnp.zeros((E, F), dtype=jnp.float32)
        w2 = jax.random.normal(ks[3], (E, F, D), dtype=jnp.float32) * (1.0 / math.sqrt(F))
        b2 = jnp.zeros((E, D), dtype=jnp.float32)
        return {'h': h, 'gate_w': gate_w, 'gate_b': gate_b, 'w1': w1, 'b1': b1, 'w2': w2, 'b2': b2}
    _L2_ffn_all = _L2_ffn_setup()
    _L2_ffn_in = {k: v for k, v in _L2_ffn_all.items() if k in ('gate_w', 'gate_b', 'w1', 'b1', 'w2', 'b2')}
    del _L2_ffn_all

    def _L3_attn_setup():
        import jax, jax.numpy as jnp
        import numpy as np
        B, N, C, H = (64, 75, 64, 8)
        STD = 0.02

        def _rel_indices(n):
            d = (jnp.arange(n)[None, :] - jnp.arange(n)[:, None]).astype(jnp.float32)
            return jnp.stack([d, jnp.zeros_like(d), d * d], axis=-1)
        key = jax.random.key(seed)
        ks = jax.random.split(key, 6)
        return {'x': jax.random.normal(ks[0], (B, N, C), jnp.float32), 'Wqk': jax.random.normal(ks[1], (2 * C, C), jnp.float32) * STD, 'Wv': jax.random.normal(ks[2], (C, C), jnp.float32) * STD, 'Wpos': jax.random.normal(ks[3], (H, 3), jnp.float32) * STD, 'bpos': jnp.zeros((H,), jnp.float32), 'Wproj': jax.random.normal(ks[4], (C, C), jnp.float32) * STD, 'bproj': jnp.zeros((C,), jnp.float32), 'gating': jnp.ones((H,), jnp.float32)}
    _L3_attn_all = _L3_attn_setup()
    _L3_attn_in = {k: v for k, v in _L3_attn_all.items() if k in ('Wqk', 'Wv', 'Wpos', 'bpos', 'Wproj', 'bproj', 'gating')}
    del _L3_attn_all

    def _L3_ffn_setup():
        import jax, jax.numpy as jnp
        import numpy as np
        B, T, D, H, E = (16, 1024, 64, 128, 8)
        key = jax.random.key(seed)
        ks = jax.random.split(key, 5)
        x = jax.random.normal(ks[0], (B, T, D), dtype=jnp.float32)
        gate_w = jax.random.normal(ks[1], (D, E), dtype=jnp.float32) * 0.02
        gate_b = jnp.zeros((E,), dtype=jnp.float32)
        W1 = jax.random.normal(ks[2], (E, D, H), dtype=jnp.float32) * 0.02
        b1 = jnp.zeros((E, H), dtype=jnp.float32)
        W2 = jax.random.normal(ks[3], (E, H, D), dtype=jnp.float32) * 0.02
        b2 = jnp.zeros((E, D), dtype=jnp.float32)
        return {'x': x, 'gate_w': gate_w, 'gate_b': gate_b, 'W1': W1, 'b1': b1, 'W2': W2, 'b2': b2}
    _L3_ffn_all = _L3_ffn_setup()
    _L3_ffn_in = {k: v for k, v in _L3_ffn_all.items() if k in ('gate_w', 'gate_b', 'W1', 'b1', 'W2', 'b2')}
    del _L3_ffn_all
    return {'x': x, 'L0_tok_w_real': _L0_tok_in['w_real'], 'L0_tok_w_imag': _L0_tok_in['w_imag'], 'L0_tok_phases': _L0_tok_in['phases'], 'L0_attn_f_in_w': _L0_attn_in['f_in_w'], 'L0_attn_f_conv_w': _L0_attn_in['f_conv_w'], 'L0_attn_f_conv_b': _L0_attn_in['f_conv_b'], 'L0_attn_f_xproj_w': _L0_attn_in['f_xproj_w'], 'L0_attn_f_dt_w': _L0_attn_in['f_dt_w'], 'L0_attn_f_dt_b': _L0_attn_in['f_dt_b'], 'L0_attn_f_A_log': _L0_attn_in['f_A_log'], 'L0_attn_f_D': _L0_attn_in['f_D'], 'L0_attn_f_out_w': _L0_attn_in['f_out_w'], 'L0_attn_b_in_w': _L0_attn_in['b_in_w'], 'L0_attn_b_conv_w': _L0_attn_in['b_conv_w'], 'L0_attn_b_conv_b': _L0_attn_in['b_conv_b'], 'L0_attn_b_xproj_w': _L0_attn_in['b_xproj_w'], 'L0_attn_b_dt_w': _L0_attn_in['b_dt_w'], 'L0_attn_b_dt_b': _L0_attn_in['b_dt_b'], 'L0_attn_b_A_log': _L0_attn_in['b_A_log'], 'L0_attn_b_D': _L0_attn_in['b_D'], 'L0_attn_b_out_w': _L0_attn_in['b_out_w'], 'L0_ffn_Wq_pk': _L0_ffn_in['Wq_pk'], 'L0_ffn_pk_keys': _L0_ffn_in['pk_keys'], 'L0_ffn_Wq': _L0_ffn_in['Wq'], 'L0_ffn_keys_table': _L0_ffn_in['keys_table'], 'L0_ffn_values_table': _L0_ffn_in['values_table'], 'L0_ffn_Wo': _L0_ffn_in['Wo'], 'L1_attn_A': _L1_attn_in['A'], 'L1_attn_B': _L1_attn_in['B'], 'L1_attn_C': _L1_attn_in['C'], 'L1_attn_h0': _L1_attn_in['h0'], 'L1_ffn_gamma': _L1_ffn_in['gamma'], 'L1_ffn_beta': _L1_ffn_in['beta'], 'L1_ffn_Wr': _L1_ffn_in['Wr'], 'L1_ffn_br': _L1_ffn_in['br'], 'L1_ffn_W1': _L1_ffn_in['W1'], 'L1_ffn_b1': _L1_ffn_in['b1'], 'L1_ffn_W2': _L1_ffn_in['W2'], 'L1_ffn_b2': _L1_ffn_in['b2'], 'L2_attn_wq': _L2_attn_in['wq'], 'L2_attn_wkv': _L2_attn_in['wkv'], 'L2_attn_wo': _L2_attn_in['wo'], 'L2_attn_q_norm_w': _L2_attn_in['q_norm_w'], 'L2_attn_k_norm_w': _L2_attn_in['k_norm_w'], 'L2_ffn_gate_w': _L2_ffn_in['gate_w'], 'L2_ffn_gate_b': _L2_ffn_in['gate_b'], 'L2_ffn_w1': _L2_ffn_in['w1'], 'L2_ffn_b1': _L2_ffn_in['b1'], 'L2_ffn_w2': _L2_ffn_in['w2'], 'L2_ffn_b2': _L2_ffn_in['b2'], 'L3_attn_Wqk': _L3_attn_in['Wqk'], 'L3_attn_Wv': _L3_attn_in['Wv'], 'L3_attn_Wpos': _L3_attn_in['Wpos'], 'L3_attn_bpos': _L3_attn_in['bpos'], 'L3_attn_Wproj': _L3_attn_in['Wproj'], 'L3_attn_bproj': _L3_attn_in['bproj'], 'L3_attn_gating': _L3_attn_in['gating'], 'L3_ffn_gate_w': _L3_ffn_in['gate_w'], 'L3_ffn_gate_b': _L3_ffn_in['gate_b'], 'L3_ffn_W1': _L3_ffn_in['W1'], 'L3_ffn_b1': _L3_ffn_in['b1'], 'L3_ffn_W2': _L3_ffn_in['W2'], 'L3_ffn_b2': _L3_ffn_in['b2']}

def reference(x, L0_tok_w_real, L0_tok_w_imag, L0_tok_phases, L0_attn_f_in_w, L0_attn_f_conv_w, L0_attn_f_conv_b, L0_attn_f_xproj_w, L0_attn_f_dt_w, L0_attn_f_dt_b, L0_attn_f_A_log, L0_attn_f_D, L0_attn_f_out_w, L0_attn_b_in_w, L0_attn_b_conv_w, L0_attn_b_conv_b, L0_attn_b_xproj_w, L0_attn_b_dt_w, L0_attn_b_dt_b, L0_attn_b_A_log, L0_attn_b_D, L0_attn_b_out_w, L0_ffn_Wq_pk, L0_ffn_pk_keys, L0_ffn_Wq, L0_ffn_keys_table, L0_ffn_values_table, L0_ffn_Wo, L1_attn_A, L1_attn_B, L1_attn_C, L1_attn_h0, L1_ffn_gamma, L1_ffn_beta, L1_ffn_Wr, L1_ffn_br, L1_ffn_W1, L1_ffn_b1, L1_ffn_W2, L1_ffn_b2, L2_attn_wq, L2_attn_wkv, L2_attn_wo, L2_attn_q_norm_w, L2_attn_k_norm_w, L2_ffn_gate_w, L2_ffn_gate_b, L2_ffn_w1, L2_ffn_b1, L2_ffn_w2, L2_ffn_b2, L3_attn_Wqk, L3_attn_Wv, L3_attn_Wpos, L3_attn_bpos, L3_attn_Wproj, L3_attn_bproj, L3_attn_gating, L3_ffn_gate_w, L3_ffn_gate_b, L3_ffn_W1, L3_ffn_b1, L3_ffn_W2, L3_ffn_b2):
    import jax
    import jax.numpy as jnp

    def _L0_tok_ref(x, w_real, w_imag, phases):
        import jax, jax.numpy as jnp
        import numpy as np
        from jax import lax
        B, S, CIN, COUT, K = (32, 512, 64, 64, 16)
        w_eff = jnp.cos(phases)[None, None, :] * w_real - jnp.sin(phases)[None, None, :] * w_imag
        y = lax.conv_general_dilated(jnp.transpose(x, (0, 2, 1)), w_eff, window_strides=(1,), padding='VALID', dimension_numbers=('NCH', 'OIH', 'NCH'))
        return jnp.transpose(y, (0, 2, 1))

    def _L0_attn_ref(g_data, f_in_w, f_conv_w, f_conv_b, f_xproj_w, f_dt_w, f_dt_b, f_A_log, f_D, f_out_w, b_in_w, b_conv_w, b_conv_b, b_xproj_w, b_dt_w, b_dt_b, b_A_log, b_D, b_out_w):
        import jax, jax.numpy as jnp
        import numpy as np
        D_MODEL = 64
        D_STATE = 16
        D_CONV = 4
        EXPAND = 2
        D_INNER = EXPAND * D_MODEL
        DT_RANK = (D_MODEL + 15) // 16
        B_SZ = 4
        SEQ = 1024

        def _mamba_params(key, prefix):
            ks = jax.random.split(key, 6)
            s = 0.02
            return {f'{prefix}_in_w': jax.random.normal(ks[0], (2 * D_INNER, D_MODEL), dtype=jnp.float32) * s, f'{prefix}_conv_w': jax.random.normal(ks[1], (D_INNER, D_CONV), dtype=jnp.float32) * s, f'{prefix}_conv_b': jnp.zeros((D_INNER,), dtype=jnp.float32), f'{prefix}_xproj_w': jax.random.normal(ks[2], (DT_RANK + 2 * D_STATE, D_INNER), dtype=jnp.float32) * s, f'{prefix}_dt_w': jax.random.normal(ks[3], (D_INNER, DT_RANK), dtype=jnp.float32) * s, f'{prefix}_dt_b': jax.random.normal(ks[4], (D_INNER,), dtype=jnp.float32) * s, f'{prefix}_A_log': jnp.log(jnp.tile(jnp.arange(1, D_STATE + 1, dtype=jnp.float32), (D_INNER, 1))), f'{prefix}_D': jnp.ones((D_INNER,), dtype=jnp.float32), f'{prefix}_out_w': jax.random.normal(ks[5], (D_MODEL, D_INNER), dtype=jnp.float32) * s}

        def _mamba(x, in_w, conv_w, conv_b, xproj_w, dt_w, dt_b, A_log, D_param, out_w):
            Bn, L, _ = x.shape
            xz = x @ in_w.T
            xin, z = jnp.split(xz, 2, axis=-1)
            lhs = xin.swapaxes(1, 2)
            rhs = conv_w[:, None, :]
            conv = jax.lax.conv_general_dilated(lhs, rhs, (1,), [(D_CONV - 1, 0)], dimension_numbers=('NCL', 'OIL', 'NCL'), feature_group_count=D_INNER)
            xc = jax.nn.silu(conv.swapaxes(1, 2) + conv_b)
            x_dbl = xc @ xproj_w.T
            dt_low = x_dbl[..., :DT_RANK]
            Bm = x_dbl[..., DT_RANK:DT_RANK + D_STATE]
            Cm = x_dbl[..., DT_RANK + D_STATE:]
            dt = jax.nn.softplus(dt_low @ dt_w.T + dt_b)
            A = -jnp.exp(A_log)

            def step(h, inps):
                dt_t, B_t, C_t, u_t = inps
                dA = jnp.exp(dt_t[:, :, None] * A)
                h = dA * h + dt_t[:, :, None] * B_t[:, None, :] * u_t[:, :, None]
                y = jnp.einsum('bdn,bn->bd', h, C_t)
                return (h, y)
            h0 = jnp.zeros((Bn, D_INNER, D_STATE), dtype=x.dtype)
            xs = (dt.swapaxes(0, 1), Bm.swapaxes(0, 1), Cm.swapaxes(0, 1), xc.swapaxes(0, 1))
            _, ys = jax.lax.scan(step, h0, xs)
            y = ys.swapaxes(0, 1) + D_param * xc
            y = y * jax.nn.silu(z)
            return y @ out_w.T
        fwd = _mamba(g_data, f_in_w, f_conv_w, f_conv_b, f_xproj_w, f_dt_w, f_dt_b, f_A_log, f_D, f_out_w)
        bwd = _mamba(jnp.flip(g_data, axis=-1), b_in_w, b_conv_w, b_conv_b, b_xproj_w, b_dt_w, b_dt_b, b_A_log, b_D, b_out_w)
        return fwd + jnp.flip(bwd, axis=-1) + g_data

    def _L0_ffn_ref(x, Wq_pk, pk_keys, Wq, keys_table, values_table, Wo):
        import jax, jax.numpy as jnp
        import numpy as np
        DIM = 64
        HEADS = 8
        NUM_KEYS = 64
        NUM_KV = NUM_KEYS ** 2
        PK_TOPK = 16
        FINAL_TOPK = 16
        DIM_KEY = DIM // 2
        P = 2

        def _pk(x, Wq_pk, pk_keys):
            b, n, _ = x.shape
            q = (x @ Wq_pk).reshape(b, n, P, HEADS, DIM_KEY).transpose(2, 0, 1, 3, 4)
            sim = jnp.einsum('pbnhd,pkhd->pbnhk', q, pk_keys)
            scores, idx = jax.lax.top_k(sim, PK_TOPK)
            idx0 = idx[0]
            idx1 = idx[1] * NUM_KEYS
            index = (idx0[..., :, None] + idx1[..., None, :]).reshape(b, n, HEADS, PK_TOPK * PK_TOPK)
            score = (scores[0][..., :, None] + scores[1][..., None, :]).reshape(b, n, HEADS, PK_TOPK * PK_TOPK)
            final_scores, pk_idx = jax.lax.top_k(score, FINAL_TOPK)
            final_indices = jnp.take_along_axis(index, pk_idx, axis=-1)
            final_scores = jax.nn.softmax(final_scores, axis=-1)
            return (final_scores, final_indices)
        b, n, d = x.shape
        q = (x @ Wq).reshape(b, n, HEADS, DIM) * DIM ** (-0.5)
        kv_scores, indices = _pk(x, Wq_pk, pk_keys)
        offsets = jnp.arange(HEADS, dtype=indices.dtype) * NUM_KV
        ind = indices + offsets[None, None, :, None]
        k = jnp.einsum('bnhk,bnhkd->bnhd', kv_scores, keys_table[ind])
        v = jnp.einsum('bnhk,bnhkd->bnhd', kv_scores, values_table[ind])
        sim = jnp.einsum('bihd,bjhd->bhij', q, k)
        neg = -jnp.finfo(sim.dtype).max
        causal = jnp.tril(jnp.ones((n, n), dtype=bool))
        sim = jnp.where(causal, sim, neg)
        attn = jax.nn.softmax(sim, axis=-1)
        out = jnp.einsum('bhij,bjhd->bhid', attn, v)
        out = out.transpose(0, 2, 1, 3).reshape(b, n, HEADS * DIM)
        return out @ Wo

    def _L1_attn_ref(inputs, A, B, C, h0):
        import jax, jax.numpy as jnp
        import numpy as np
        STATE_DIM = 64
        INPUT_DIM = 64
        OUTPUT_DIM = 64
        BATCH = 16
        SEQ_LEN = 1024
        batch = inputs.shape[0]
        Bu = jnp.einsum('bti,is->bts', inputs, B)
        Bu_t = jnp.swapaxes(Bu, 0, 1)

        def step(h, bu):
            h = h * A + bu
            return (h, h)
        h_init = jnp.broadcast_to(h0, (batch, h0.shape[0]))
        _, hs = jax.lax.scan(step, h_init, Bu_t)
        ys = jnp.einsum('tbs,so->bto', hs, C)
        return ys

    def _L1_ffn_ref(x, gamma, beta, Wr, br, W1, b1, W2, b2):
        import jax, jax.numpy as jnp
        import numpy as np
        E = 8
        K = 2
        D = 64
        H = 128
        DOUT = 64
        EPS = 1e-05
        mu = jnp.mean(x, axis=-1, keepdims=True)
        var = jnp.mean(jnp.square(x - mu), axis=-1, keepdims=True)
        xn = (x - mu) * jax.lax.rsqrt(var + EPS) * gamma + beta
        logits = jnp.einsum('bsd,de->bse', xn, Wr) + br
        top_vals, top_idx = jax.lax.top_k(logits, K)
        w = jax.nn.softmax(top_vals, axis=-1)
        w_full = jnp.einsum('bsk,bske->bse', w, jax.nn.one_hot(top_idx, E, dtype=w.dtype))
        y = jnp.zeros(x.shape[:-1] + (DOUT,), x.dtype)
        for e in range(E):
            h = jax.nn.gelu(jnp.einsum('bsd,dh->bsh', xn, W1[e]) + b1[e], approximate=False)
            y_e = jnp.einsum('bsh,hd->bsd', h, W2[e]) + b2[e]
            y = y + y_e * w_full[..., e, None]
        return y

    def _L2_attn_ref(x, wq, wkv, wo, q_norm_w, k_norm_w):
        import jax, jax.numpy as jnp
        import numpy as np
        import math
        B, T, D_MODEL = (1, 512, 64)
        N_Q, N_KV = (16, 1)
        D_HEAD = D_MODEL // N_KV
        QPG = N_Q // N_KV
        ROPE_BASE = 10000.0
        WINDOW = 128
        EPS = 1.1920929e-07
        NEG = -1e+30

        def _rope(x, base=ROPE_BASE):
            t, d = (x.shape[-2], x.shape[-1])
            freqs = base ** (-2.0 * jnp.arange(d // 2, dtype=jnp.float32) / d)
            theta = jnp.arange(t, dtype=jnp.float32)[:, None] * freqs[None, :]
            cos, sin = (jnp.cos(theta), jnp.sin(theta))
            x1, x2 = (x[..., 0::2], x[..., 1::2])
            r1 = x1 * cos - x2 * sin
            r2 = x1 * sin + x2 * cos
            return jnp.stack([r1, r2], axis=-1).reshape(x.shape)

        def _rmsnorm(x, w):
            return x * jax.lax.rsqrt(jnp.mean(x * x, axis=-1, keepdims=True) + EPS) * w
        Bx, Tx, C = x.shape
        q = x @ wq.T
        kv = x @ wkv.T
        k, v = (kv[..., :N_KV * D_HEAD], kv[..., N_KV * D_HEAD:])
        q = q.reshape(Bx, Tx, QPG, N_KV, D_HEAD).transpose(0, 2, 3, 1, 4)
        k = k.reshape(Bx, Tx, 1, N_KV, D_HEAD).transpose(0, 2, 3, 1, 4)
        v = v.reshape(Bx, Tx, 1, N_KV, D_HEAD).transpose(0, 2, 3, 1, 4)
        q = _rmsnorm(_rope(q), q_norm_w)
        k = _rmsnorm(_rope(k), k_norm_w)
        rows = jnp.arange(Tx)[:, None]
        cols = jnp.arange(Tx)[None, :]
        mask = (cols <= rows) & (rows - cols <= WINDOW)
        scale = 1.0 / math.sqrt(D_HEAD)
        scores = jnp.einsum('bqgtd,bqgsd->bqgts', q, k) * scale
        scores = jnp.where(mask[None, None, None], scores, NEG)
        attn = jax.nn.softmax(scores, axis=-1)
        out = jnp.einsum('bqgts,bqgsd->bqgtd', attn, v)
        out = out.transpose(0, 3, 1, 2, 4).reshape(Bx, Tx, QPG * N_KV * D_HEAD)
        return out @ wo.T

    def _L2_ffn_ref(h, gate_w, gate_b, w1, b1, w2, b2):
        import math
        import jax, jax.numpy as jnp
        import numpy as np
        CAPACITY_FACTOR = 1.25
        B, L, D = h.shape
        E = gate_w.shape[1]
        T = B * L
        C = max(1, math.ceil(CAPACITY_FACTOR * T / E))
        x = h.reshape(T, D)
        logits = x @ gate_w + gate_b
        probs = jax.nn.softmax(logits, axis=-1)
        idx = jnp.argmax(probs, axis=-1)
        prb = jnp.take_along_axis(probs, idx[:, None], axis=1)[:, 0]
        one_hot = jax.nn.one_hot(idx, E, dtype=jnp.float32)
        pos = (jnp.cumsum(one_hot, axis=0) * one_hot).sum(-1).astype(jnp.int32) - 1
        kept = pos < C
        pos_safe = jnp.where(kept, pos, C)
        buf = jnp.zeros((E, C, D), dtype=h.dtype).at[idx, pos_safe].set(x, mode='drop')
        hmid = jax.nn.relu(jnp.einsum('ecd,edf->ecf', buf, w1) + b1[:, None, :])
        ybuf = jnp.einsum('ecf,efd->ecd', hmid, w2) + b2[:, None, :]
        pos_g = jnp.minimum(pos, C - 1)
        y_tok = ybuf[idx, pos_g] * (prb * kept)[:, None]
        y = y_tok.reshape(B, L, D)
        y = jnp.nan_to_num(y, nan=0.0, posinf=10000.0, neginf=-10000.0)
        return y

    def _L3_attn_ref(x, Wqk, Wv, Wpos, bpos, Wproj, bproj, gating):
        import jax, jax.numpy as jnp
        import numpy as np
        B, N, C, H = (64, 75, 64, 8)
        STD = 0.02

        def _rel_indices(n):
            d = (jnp.arange(n)[None, :] - jnp.arange(n)[:, None]).astype(jnp.float32)
            return jnp.stack([d, jnp.zeros_like(d), d * d], axis=-1)
        Bb, Nn, Cc = x.shape
        Hh = gating.shape[0]
        hd = Cc // Hh
        scale = hd ** (-0.5)
        qk = (x @ Wqk.T).reshape(Bb, Nn, 2, Hh, hd)
        q = qk[:, :, 0].transpose(0, 2, 1, 3)
        k = qk[:, :, 1].transpose(0, 2, 1, 3)
        patch_score = jax.nn.softmax(jnp.einsum('bhnd,bhmd->bhnm', q, k) * scale, axis=-1)
        rel = _rel_indices(Nn)
        pos_score = (rel @ Wpos.T + bpos).transpose(2, 0, 1)
        pos_score = jax.nn.softmax(pos_score, axis=-1)
        g = jax.nn.sigmoid(gating)[None, :, None, None]
        attn = (1.0 - g) * patch_score + g * pos_score[None]
        attn = attn / attn.sum(axis=-1, keepdims=True)
        v = (x @ Wv.T).reshape(Bb, Nn, Hh, hd).transpose(0, 2, 1, 3)
        out = jnp.einsum('bhnm,bhmd->bhnd', attn, v)
        out = out.transpose(0, 2, 1, 3).reshape(Bb, Nn, Cc)
        return out @ Wproj.T + bproj

    def _L3_ffn_ref(x, gate_w, gate_b, W1, b1, W2, b2):
        import jax, jax.numpy as jnp
        import numpy as np
        B, T, D, H, E = (16, 1024, 64, 128, 8)
        Bb, Tt, Dd = x.shape
        Ee = gate_w.shape[1]
        xf = x.reshape(-1, Dd)
        N = xf.shape[0]
        logits = xf @ gate_w + gate_b
        probs = jax.nn.softmax(logits, axis=-1)
        top2_vals, top2_idx = jax.lax.top_k(probs, 2)
        cw = jnp.zeros((N, Ee), dtype=xf.dtype).at[jnp.arange(N)[:, None], top2_idx].add(top2_vals)

        def step(acc, params):
            w1, bb1, w2, bb2, we = params
            h = jax.nn.gelu(xf @ w1 + bb1, approximate=False)
            y = h @ w2 + bb2
            return (acc + we[:, None] * y, None)
        out, _ = jax.lax.scan(step, jnp.zeros_like(xf), (W1, b1, W2, b2, cw.T))
        return out.reshape(Bb, Tt, Dd)
    h = _L0_tok_ref(x, L0_tok_w_real, L0_tok_w_imag, L0_tok_phases)
    h = h + _L0_attn_ref(_layernorm(h, axis=-1), L0_attn_f_in_w, L0_attn_f_conv_w, L0_attn_f_conv_b, L0_attn_f_xproj_w, L0_attn_f_dt_w, L0_attn_f_dt_b, L0_attn_f_A_log, L0_attn_f_D, L0_attn_f_out_w, L0_attn_b_in_w, L0_attn_b_conv_w, L0_attn_b_conv_b, L0_attn_b_xproj_w, L0_attn_b_dt_w, L0_attn_b_dt_b, L0_attn_b_A_log, L0_attn_b_D, L0_attn_b_out_w)
    h = h + _L0_ffn_ref(_layernorm(h, axis=-1), L0_ffn_Wq_pk, L0_ffn_pk_keys, L0_ffn_Wq, L0_ffn_keys_table, L0_ffn_values_table, L0_ffn_Wo)
    h = h + _L1_attn_ref(_layernorm(h, axis=-1), L1_attn_A, L1_attn_B, L1_attn_C, L1_attn_h0)
    h = h + _L1_ffn_ref(_layernorm(h, axis=-1), L1_ffn_gamma, L1_ffn_beta, L1_ffn_Wr, L1_ffn_br, L1_ffn_W1, L1_ffn_b1, L1_ffn_W2, L1_ffn_b2)
    h = h + _L2_attn_ref(_layernorm(h, axis=-1), L2_attn_wq, L2_attn_wkv, L2_attn_wo, L2_attn_q_norm_w, L2_attn_k_norm_w)
    h = h + _L2_ffn_ref(_layernorm(h, axis=-1), L2_ffn_gate_w, L2_ffn_gate_b, L2_ffn_w1, L2_ffn_b1, L2_ffn_w2, L2_ffn_b2)
    h = h + _L3_attn_ref(_layernorm(h, axis=-1), L3_attn_Wqk, L3_attn_Wv, L3_attn_Wpos, L3_attn_bpos, L3_attn_Wproj, L3_attn_bproj, L3_attn_gating)
    h = h + _L3_ffn_ref(_layernorm(h, axis=-1), L3_ffn_gate_w, L3_ffn_gate_b, L3_ffn_W1, L3_ffn_b1, L3_ffn_W2, L3_ffn_b2)
    return h

_drawn_inputs = setup_inputs


def setup_inputs(seed=0):
    import zlib

    import numpy as np

    out = dict(_drawn_inputs(seed))
    spreads = {'L0_attn_f_conv_b': (0.0, 0.8),
     'L0_attn_f_D': (1.0, 0.6),
     'L0_attn_b_conv_b': (0.0, 0.8),
     'L0_attn_b_D': (1.0, 0.6),
     'L1_attn_h0': (0.0, 0.8),
     'L1_ffn_br': (0.0, 0.8),
     'L2_attn_q_norm_w': (1.0, 0.6),
     'L2_attn_k_norm_w': (1.0, 0.6),
     'L2_ffn_gate_b': (0.0, 0.321),
     'L2_ffn_b1': (0.0, 2.0),
     'L2_ffn_b2': (0.0, 2.0),
     'L3_attn_bpos': (0.0, 2.0),
     'L3_attn_bproj': (0.0, 0.927),
     'L3_attn_gating': (1.0, 0.6),
     'L3_ffn_gate_b': (0.0, 0.8),
     'L3_ffn_b1': (0.0, 0.8),
     'L3_ffn_b2': (0.0, 0.8)}
    factors = {'L0_attn_f_in_w': 8.0,
     'L0_attn_f_conv_w': 8.0,
     'L0_attn_f_xproj_w': 8.0,
     'L0_attn_f_dt_w': 8.0,
     'L0_attn_f_dt_b': 8.0,
     'L0_attn_f_A_log': 8.0,
     'L0_attn_f_out_w': 8.0,
     'L0_attn_b_in_w': 8.0,
     'L0_attn_b_conv_w': 8.0,
     'L0_attn_b_xproj_w': 8.0,
     'L0_attn_b_dt_w': 8.0,
     'L0_attn_b_dt_b': 8.0,
     'L0_attn_b_A_log': 8.0,
     'L0_attn_b_out_w': 8.0,
     'L0_ffn_Wq_pk': 8.0,
     'L0_ffn_pk_keys': 24.317,
     'L0_ffn_Wq': 64.0,
     'L0_ffn_keys_table': 64.0,
     'L0_ffn_values_table': 25.122,
     'L0_ffn_Wo': 8.0,
     'L1_ffn_gamma': 8.0,
     'L1_ffn_beta': 8.0,
     'L1_ffn_Wr': 8.0,
     'L1_ffn_W1': 8.0,
     'L1_ffn_b1': 27.408,
     'L1_ffn_W2': 8.0,
     'L1_ffn_b2': 35.361,
     'L2_attn_wq': 8.0,
     'L2_attn_wkv': 8.0,
     'L2_attn_wo': 8.0,
     'L2_ffn_gate_w': 2.964,
     'L2_ffn_w1': 3.11,
     'L3_attn_Wqk': 40.72,
     'L3_attn_Wv': 8.0,
     'L3_attn_Wpos': 8.0,
     'L3_attn_Wproj': 8.0,
     'L3_ffn_gate_w': 8.0,
     'L3_ffn_W1': 8.0,
     'L3_ffn_W2': 8.0}
    for name, (base, spread) in spreads.items():
        noise = np.random.default_rng([zlib.crc32(name.encode()), seed]).standard_normal(out[name].shape)
        drawn = base * np.exp(spread * noise) if base else spread * noise
        out[name] = jnp.asarray(drawn.astype(out[name].dtype))
    for name, factor in factors.items():
        out[name] = (out[name] * factor).astype(out[name].dtype)
    return out
```

```python
import numpy as np

import concourse.bass as bass
from concourse import mybir
from concourse.alu_op_type import AluOpType as ALU

ACT = mybir.ActivationFunctionType
AX = mybir.AxisListType
F32 = mybir.dt.float32
BF16 = mybir.dt.bfloat16
U32 = mybir.dt.uint32
I32 = mybir.dt.int32

P = 128
B = 4
S_IN = 750
TAPS = 16
T = S_IN - TAPS + 1
NT = -(-T // P)
TP = NT * P
TAIL = T - (NT - 1) * P
TW = 736
D = 64
XC = TP + TAPS + 1
LN_EPS = 1e-5
BIG = 3.0e38
FMAX = 3.4028235e38

DI, DS, DTR, DC = 128, 16, 4, 4
PH, NK, DK, TOPK = 8, 64, 32, 16
NKV = NK * NK
ROW = [TOPK // (a + 1) for a in range(TOPK)]
START = [sum(ROW[:a]) for a in range(TOPK)]
NCAND = sum(ROW)
GROUPS = [(a, ROW.count(ROW[a]), ROW[a]) for a in range(TOPK) if a == 0 or ROW[a] != ROW[a - 1]]
E = 8
CAP = -(-5 * B * T // (4 * E))
QH, WINDOW = 16, 128
RMS_EPS = 1.1920929e-07
GH, GD = 8, 8
DOFF = (NT - 1) * P
DCOLS = DOFF + T


def weight_layout():
    w = {"ident": (P, P), "cos": (P, TP), "sin": (P, TP), "masks": (P, 2 * P), "blockones": (P, P),
         "ones": (P, P), "tri": (P, P), "iota": (P, 64), "headoff": (P, PH * TOPK), "valid": (P, NT),
         "bsel": (96, 32)}
    for d in "fb":
        w |= {d + "_in": (D, 2 * DI), d + "_cw": (DI, DC), d + "_cb": (DI, 1), d + "_xp": (DI, DTR + 2 * DS),
              d + "_dtw": (DTR, DI), d + "_dtb": (DI, 1), d + "_alog": (DI, DS), d + "_D": (DI, 1), d + "_out": (DI, D)}
    w |= {"pk_wq": (D, PH * D), "pk_wo": (P, 4 * D)}
    w |= {"ssm_A": (D, 1), "ssm_h0": (D, 1), "ssm_B": (D, D), "ssm_C": (D, D)}
    w |= {"gamma": (P, D), "beta": (P, D)}
    for m, f in (("m1", 128), ("m2", 256), ("m3", 128)):
        w |= {m + "_g": (D + 1, E), m + "_w1": (D, E * f), m + "_b1": (P, E * f // P), m + "_w2": (P, E * f // P * D),
              m + "_b2": (1, E * D)}
    w |= {"wa_q": (D, QH * D), "wa_qs": (D, QH * D), "wa_k": (D, P), "wa_ks": (D, P), "wa_v": (D, D),
          "wa_qn": (P, 1), "wa_kn": (P, 1), "wa_o": (P, QH * D * D // P)}
    w |= {"ga_q": (D, 2 * P), "ga_k": (D, 2 * P), "ga_v": (D, D), "ga_wpos": (P, GH * 3), "ga_bpos": (P, GH),
          "ga_g": (P, GH), "ga_o": (D, D), "ga_ob": (P, D)}
    return w


def setup_layout():
    return {"cv_r": (P, TAPS // 2 * D), "cv_i": (P, TAPS // 2 * D), "cv_ph": (P, TAPS // 2),
            "pk_q": (DK, 2 * PH * D), "pk_k": (DK, 2 * PH * NK)}


def columns(layout):
    at, place = 0, {}
    for name, (rows, cols) in layout.items():
        place[name] = (rows, at, cols)
        at += cols
    return place, at


class Core:

    def __init__(self, nc):
        self.nc = nc
        self.place, total = columns(weight_layout())
        self.w = nc.alloc_sbuf_tensor("weights", [P, total], F32)
        self.ps = nc.alloc_psum_tensor("psum", [P, 8, 512], F32)
        self.kept = {}
        self.last = None

        def sb(name, shape, dt=F32):
            return nc.alloc_sbuf_tensor(name, shape, dt)

        self.identb = sb("ident_bf16", [P, P], BF16)
        self.masksb = sb("masks_bf16", [P, 2 * P], BF16)
        self.bselb = sb("bc_selector", [96, 32], BF16)
        self.convw = sb("conv_weight", [P, TAPS // 2, D])
        self.fold = sb("folded_keys", [D, 2, PH, NK])
        self.An = sb("minus_exp_A", [DI, 2, DS])
        self.omg = sb("one_minus_gate", [P, GH])
        self.sg = sb("gate", [P, GH])
        self.knw = sb("key_norm_weight", [P, 1])
        self.carry = sb("assigned_before", [P, E])
        self.h = sb("hidden", [P, NT, D])
        self.sq = sb("squares", [P, NT, D])
        self.y = sb("normed", [P, NT, D])
        self.yT = sb("normed_T", [D + 1, TP])
        self.st = sb("ln_stats", [P, 8, NT])
        self.hall = sb("hidden_of_batches", [P, B, NT * D])
        self.vall = sb("gated_v_of_batches", [P, NT, GH, B, GD])
        self.poss = sb("positional_sum", [P, NT, GH])
        self.arena = sb("arena", [P, ARENA])
        self.at = 0
        self.kv = sb("gathered", [P, NT, 2, PH * D])
        self.poso = self.kv[:, :, :, :].rearrange("p t s n -> p (t s n)")[:, 0:B * NT * D].rearrange(
            "p (b t d) -> p b t d", b=B, t=NT)
        self.pv = sb("product_values", [P, NT, PH * D])
        n = NT * PH * TOPK
        self.idx, self.idx_next = sb("rows", [P, n], I32), sb("rows_next", [P, 2, n], I32)
        self.wgt, self.wgt_next = sb("row_weights", [P, n]), sb("row_weights_next", [P, 2, n])
        self.fetch = Fetch(self)

    def W(self, name):
        rows, at, cols = self.place[name]
        return self.w[0:rows, at:at + cols]

    def take(self, cols, rows=P, dt=F32):
        at = self.at
        self.at += cols
        assert self.at <= ARENA, (self.at, ARENA)
        v = self.arena[0:rows, at:at + cols]
        return v if dt == F32 else v.bitcast(dt)

    def free(self, at=0):
        self.at = at

    def sems(self, stage, names):
        if stage not in self.kept:
            self.kept[stage] = [self.nc.alloc_semaphore(f"{stage}_{n}") for n in names]
        return self.kept[stage]

    def clear(self, pool, *stages):
        for s in stages:
            if s and self.kept[s]:
                pool.sem_clear(range(self.kept[s][0].num, self.kept[s][-1].num + 1))


ARENA = 12224


def one(b):
    return bass.ds(b, 1)


HALF = TOPK // 2
SLOTS = 4
LEAD = 2


class Fetch:

    def __init__(self, c):
        self.c = c
        self.rows = [c.nc.alloc_sbuf_tensor(f"fetched_{s}", [P, HALF, 2 * D], F32) for s in range(SLOTS)]
        self.part = c.nc.alloc_sbuf_tensor("fetched_sum", [P, 2 * D], F32)
        self.landed = [c.nc.alloc_semaphore(f"rows_landed_{s}") for s in range(SLOTS)]
        self.used, self.chain = c.nc.alloc_semaphore("rows_used"), c.nc.alloc_semaphore("rows_chain")
        self.total = 2 * NT * PH
        self.eaten = 0
        self.active = False

    def start(self, table, every):
        self.table, self.active, self.every = table, True, every
        self.started = self.eaten = self.links = 0
        self.credit = 0.0

    def limit(self):
        return min(self.total, self.eaten + LEAD) * HALF if self.active else 0

    def issue(self, pool, upto, most=1 << 30):
        c = self.c
        while self.active and self.started < upto and most:
            f, k = divmod(self.started, HALF)
            s = f % SLOTS
            if f >= SLOTS and k == 0:
                pool.wait_ge(self.used, f - SLOTS + 1)
            n = f // 2 * TOPK + f % 2 * HALF + k
            pool.indirect_dma_start(self.rows[s][:, k, :], None, self.table,
                                    bass.IndirectOffsetOnAxis(ap=c.idx[:, n:n + 1], axis=0)).then_inc(self.landed[s], 16)
            self.started += 1
            most -= 1

    def hook(self, dve, us):
        if not self.active:
            return
        self.credit += us
        while self.credit >= self.every and self.eaten < self.total:
            self.credit -= self.every
            self.eat(dve)

    def link(self, dve, ins):
        self.links += 1
        ins.then_inc(self.chain, 1)
        dve.wait_ge(self.chain, self.links)

    def eat(self, dve):
        c, nc, f = self.c, self.c.nc, self.eaten
        s, (i, h) = f % SLOTS, divmod(f // 2, PH)
        n = f // 2 * TOPK + f % 2 * HALF
        r = self.rows[s][:, :, :]
        dve.wait_ge(self.landed[s], 16 * HALF * (f // SLOTS + 1))
        self.link(dve, nc.vector.tensor_tensor(r, r, bc(c.wgt[:, n:n + HALF], [P, HALF, 2 * D], 2), ALU.mult))
        o = c.kv[:, i, :, h * D:(h + 1) * D]
        rs = r.rearrange("p k (s d) -> p s d k", s=2)
        part = self.part[:, :].rearrange("p (s d) -> p s d", s=2)
        nc.vector.tensor_reduce(part if f % 2 else o, rs, AX.X, ALU.add).then_inc(self.used, 1)
        if f % 2:
            dve.wait_ge(self.used, f + 1)
            self.link(dve, nc.vector.tensor_tensor(o, o, part, ALU.add))
        self.eaten += 1

    def finish(self):
        c = self.c
        with c.nc.Block() as block:
            @block.vector
            def _(dve):
                while self.eaten < self.total:
                    self.eat(dve)

            @block.gpsimd
            def _(pool):
                c.clear(pool, c.last)
                self.issue(pool, self.total * HALF)
                for s in range(SLOTS):
                    pool.wait_ge(self.landed[s], 16 * HALF * (self.total // SLOTS))
        with c.nc.Block() as block:
            @block.gpsimd
            def _(pool):
                pool.dma_reset(range(self.landed[0].num, self.landed[-1].num + 1))
                pool.sem_clear(range(self.landed[0].num, self.chain.num + 1))
        c.last = None
        self.active = False


def linker(eng, sem, start=0):
    n = [start]

    def link(ins):
        n[0] += 1
        ins.then_inc(sem, 1)
        eng.wait_ge(sem, n[0])
    return link


def bc(ap, shape, axis):
    return ap.unsqueeze(axis).to_broadcast(shape)



def setup(c, weights, raw):
    nc = c.nc
    place, total = columns(setup_layout())
    c.free()
    rw = c.take(total)

    def R(name):
        rows, at, cols = place[name]
        return rw[0:rows, at:at + cols]

    tr = [c.take(TAPS // 2) for _ in range(6)]
    tmp = c.take(TAPS // 2 * D)
    loaded, chain, trig, folded, anz, gz = c.sems("setup", ["loaded", "chain", "trig", "folded", "A", "gate"])
    with nc.Block() as block:
        @block.sync
        def _(sp):
            sp.dma_start(rw[:, :], raw).then_inc(loaded, 16)
            sp.dma_start(c.w[:, :], weights).then_inc(loaded, 16)

        @block.scalar
        def _(act):
            act.wait_ge(loaded, 32)
            for k, d in enumerate("fb"):
                act.activation(c.An[:, k, :], c.W(d + "_alog"), ACT.Exp).then_inc(anz, 1)
            act.activation(c.sg[:, :], c.W("ga_g"), ACT.Sigmoid).then_inc(gz, 1)
            act.wait_ge(trig, 1)
            act.activation(tr[2], tr[0], ACT.Sin, scale=TWO_PI).then_inc(trig, 1)
            act.activation(tr[3], tr[1], ACT.Sin, scale=TWO_PI).then_inc(trig, 1)

        @block.vector
        def _(dve):
            link = linker(dve, chain)
            dve.wait_ge(loaded, 32)
            for k, quarter in enumerate((0.0, 0.25)):
                link(nc.vector.tensor_scalar(tr[k], R("cv_ph"), 1.0 / TWO_PI, quarter, ALU.mult, ALU.add))
                link(nc.vector.tensor_scalar(tr[4], tr[k], ROUND, None, ALU.add))
                link(nc.vector.tensor_scalar(tr[5], tr[4], ROUND, None, ALU.subtract))
                link(nc.vector.tensor_tensor(tr[4], tr[k], tr[5], ALU.subtract))
                link(nc.vector.tensor_scalar(tr[k], tr[4], 0.4999999, -0.4999999, ALU.min, ALU.max))
            nc.vector.tensor_copy(c.identb[:, :], c.W("ident")).then_inc(trig, 1)
            link(nc.vector.tensor_copy(c.masksb[:, :], c.W("masks")))
            link(nc.vector.tensor_copy(c.bselb[:, :], c.W("bsel")))
            link(nc.vector.memset(c.yT[D:D + 1, :], 1.0))
            link(nc.vector.memset(c.carry[:, :], 0.0))
            link(nc.vector.tensor_tensor(c.knw[:, :], c.W("wa_qn"), c.W("wa_kn"), ALU.mult))
            dve.wait_ge(anz, 2)
            link(nc.vector.tensor_scalar(c.An[:, :, :], c.An[:, :, :], -1.0, None, ALU.mult))
            dve.wait_ge(gz, 1)
            link(nc.vector.tensor_scalar(c.omg[:, :], c.sg[:, :], -1.0, 1.0, ALU.mult, ALU.add))
            dve.wait_ge(trig, 3)
            shape = [P, TAPS // 2, D]
            wr = R("cv_r").rearrange("p (m o) -> p m o", o=D)
            wi = R("cv_i").rearrange("p (m o) -> p m o", o=D)
            t3 = tmp.rearrange("p (m o) -> p m o", o=D)
            link(nc.vector.tensor_tensor(c.convw[:, :, :], wr, bc(tr[3], shape, 2), ALU.mult))
            link(nc.vector.tensor_tensor(t3, wi, bc(tr[2], shape, 2), ALU.mult))
            link(nc.vector.tensor_tensor(c.convw[:, :, :], c.convw[:, :, :], t3, ALU.subtract))
            dve.wait_ge(folded, 1)
            for k in range(2):
                link(nc.vector.tensor_copy(c.fold[:, k, :, :].rearrange("p h k -> p (h k)"), c.ps[0:D, k, :]))

        @block.tensor
        def _(pe):
            pe.wait_ge(loaded, 32)
            for n in range(2 * PH):
                last = pe.matmul(c.ps[0:D, n // PH, n % PH * NK:(n % PH + 1) * NK], R("pk_q")[:, n * D:(n + 1) * D],
                                 R("pk_k")[:, n * NK:(n + 1) * NK], start=True, stop=True)
            last.then_inc(folded, 1)
    c.last = "setup"


TWO_PI = 6.283185307179586
ROUND = 12582912.0



def conv(c, x, b):
    nc = c.nc
    c.free()
    xT = c.take(XC)
    loaded, made = c.sems("conv", ["loaded", "made"])
    with nc.Block() as block:
        @block.sync
        def _(sp):
            sp.dma_start(xT[:, 0:XC - 1], x[bass.ds(b * P, P), :]).then_inc(loaded, 16)

        @block.tensor
        def _(pe):
            pe.wait_ge(loaded, 16)
            for i in range(NT):
                for m in range(TAPS // 2):
                    last = pe.matmul(c.ps[:, 0, i * D:(i + 1) * D], xT[:, i * P + 2 * m:(i + 1) * P + 2 * m],
                                     c.convw[:, m, :], start=(m == 0), stop=(m == TAPS // 2 - 1))
            last.then_inc(made, 1)

        @block.vector
        def _(dve):
            c.fetch.hook(dve, 8)
            c.fetch.hook(dve, 8)
            dve.wait_ge(made, 1)
            nc.vector.tensor_copy(c.h[:, :, :].rearrange("p t d -> p (t d)"), c.ps[:, 0, 0:NT * D])

        @block.gpsimd
        def _(pool):
            c.clear(pool, c.last)
            c.fetch.issue(pool, c.fetch.limit())
    c.last = "conv"



def norm(c, src, affine=None, stage="ln"):
    nc = c.nc
    chain, var, root, normed, turned = c.sems(stage, ["chain", "var", "root", "normed", "turned"])
    full = [P, NT, D]
    s, mean, v, std, r = (c.st[:, k, :] for k in range(5))
    sq = c.sq[:, :, :]
    with nc.Block() as block:
        @block.vector
        def _(dve):
            link = linker(dve, chain)
            link(nc.vector.reduce_sum(s, src, AX.X))
            link(nc.vector.tensor_scalar(mean, s, 1.0 / D, None, ALU.mult))
            link(nc.vector.tensor_tensor(c.y[:, :, :], src, bc(mean, full, 2), ALU.subtract))
            link(nc.vector.tensor_tensor(sq, c.y[:, :, :], c.y[:, :, :], ALU.mult))
            link(nc.vector.reduce_sum(s, sq, AX.X))
            nc.vector.tensor_scalar(v, s, 1.0 / D, LN_EPS, ALU.mult, ALU.add).then_inc(var, 1)
            dve.wait_ge(root, 1)
            link(nc.vector.reciprocal(r, std))
            if affine:
                link(nc.vector.tensor_tensor(c.y[:, :, :], c.y[:, :, :], bc(r, full, 2), ALU.mult))
                link(nc.vector.tensor_tensor(c.y[:, :, :], c.y[:, :, :], bc(affine[0], full, 1), ALU.mult))
                nc.vector.tensor_tensor(c.y[:, :, :], c.y[:, :, :], bc(affine[1], full, 1), ALU.add).then_inc(normed, 1)
            else:
                nc.vector.tensor_tensor(c.y[:, :, :], c.y[:, :, :], bc(r, full, 2), ALU.mult).then_inc(normed, 1)
            c.fetch.hook(dve, 5)

        @block.tensor
        def _(pe):
            pe.wait_ge(normed, 1)
            for i in range(NT):
                last = pe.transpose(c.ps[0:D, i // 4, i % 4 * P:(i % 4 + 1) * P], c.y[:, i, :], c.W("ident"))
                if i in (3, NT - 1):
                    last.then_inc(turned, 1)

        @block.scalar
        def _(act):
            act.wait_ge(var, 1)
            nc.scalar.activation(std, v, ACT.Sqrt).then_inc(root, 1)
            for k, (lo, hi) in enumerate(((0, 4), (4, NT))):
                act.wait_ge(turned, k + 1)
                nc.scalar.activation(c.yT[0:D, lo * P:hi * P], c.ps[0:D, k, 0:(hi - lo) * P], ACT.Copy)

        @block.gpsimd
        def _(pool):
            c.clear(pool, c.last)
            c.fetch.issue(pool, c.fetch.limit())
    c.last = stage



def mamba(c):
    nc = c.nc
    c.free()
    H = TW // 2
    xin = c.take(DC - 1 + TW)
    xc, sz, dt, dtx = (c.take(TW) for _ in range(4))
    bcb = c.take(TW // 2, 96, BF16)
    dA = [c.take(TW) for _ in range(2)]
    dBu = [c.take(TW) for _ in range(2)]
    hs = [c.take(TW) for _ in range(2)]
    hc = [c.take(TW) for _ in range(2)]
    yacc = c.take(TW)
    yd = [c.take(TP) for _ in range(2)]
    ea, eb, ec, ed, v = *dA, *dBu, hs[0]
    dlow, r1, r2 = hs[1][0:DTR, :], hc[0][0:32, :], hc[1][0:32, :]
    mid = hs[0][0:32, 0:TW // 2].bitcast(BF16)
    (chain, padded, projected, evacuated, convolved, activated, low, lowcopied, dtproj, soft, dtready,
     split, bready, cready, decay, inp, state, outp, summed, gated, aready, prod) = c.sems("mamba", [
         "chain", "padded", "projected", "evacuated", "convolved", "activated", "low", "lowcopied", "dtproj",
         "soft", "dtready", "split", "bready", "cready", "decay", "inp", "state", "outp", "summed", "gated",
         "aready", "prod"])

    def two(bank, rows=P):
        return c.ps[0:rows, bank:bank + 2, 0:H]

    def halves(v, rows=P):
        return v.rearrange("p (s n) -> p s n", s=2)

    sums = []
    with nc.Block() as block:
        @block.tensor
        def _(pe):
            for k, d in enumerate("fb"):
                if k:
                    pe.wait_ge(outp, DS)
                for z in range(2):
                    for s in range(2):
                        last = pe.matmul(c.ps[:, 2 * z + s, 0:H], c.W(d + "_in")[:, z * DI:(z + 1) * DI],
                                         c.yT[0:D, s * H:(s + 1) * H], start=True, stop=True)
                    last.then_inc(projected, 1)
                pe.wait_ge(activated, 2 * k + 2)
                for s in range(2):
                    pe.matmul(c.ps[0:DTR, 4 + s, 0:H], c.W(d + "_xp")[:, 0:DTR], xc[:, s * H:(s + 1) * H],
                              start=True, stop=True)
                for s in range(2):
                    last = pe.matmul(c.ps[0:32, 6 + s, 0:H], c.W(d + "_xp")[:, DTR:DTR + 2 * DS],
                                     xc[:, s * H:(s + 1) * H], start=True, stop=True)
                last.then_inc(low, 1)
                pe.wait_ge(lowcopied, k + 1)
                for s in range(2):
                    last = pe.matmul(c.ps[:, s, 0:H], c.W(d + "_dtw"), dlow[:, s * H:(s + 1) * H], start=True, stop=True)
                last.then_inc(dtproj, 1)
                pe.wait_ge(split, k + 1)
                for n in range(DS):
                    g = k * DS + n
                    o = 4 * (g % 2)
                    if n == 0:
                        pe.wait_ge(soft, k + 1)
                        pe.wait_ge(aready, 3 * k + 1)
                    if n >= 2 or k:
                        pe.wait_ge(outp, g - 1)
                    for z, ready in ((0, bready), (1, cready)):
                        for s in range(2):
                            last = pe.matmul(c.ps[:, o + 2 * z + s, 0:H],
                                             c.bselb[:, z * DS + n:z * DS + n + 1].to_broadcast([96, P]),
                                             bcb[:, s * H:(s + 1) * H], start=True, stop=True)
                        last.then_inc(ready, 1)
            pe.wait_ge(gated, 2)
            pe.wait_ge(outp, 2 * DS)
            for i in range(NT):
                for k, d in enumerate("fb"):
                    last = pe.matmul(c.ps[:, 0, i * D:(i + 1) * D], yd[k][:, i * P:(i + 1) * P], c.W(d + "_out"),
                                     start=(k == 0), stop=(k == 1))
            last.then_inc(prod, 1)

        @block.scalar
        def _(act):
            for k, d in enumerate("fb"):
                act.wait_ge(projected, 2 * k + 1)
                if k:
                    act.wait_ge(convolved, 3)
                    act.wait_ge(gated, 1)
                nc.scalar.activation(halves(xin[:, DC - 1:]), two(0), ACT.Copy).then_inc(evacuated, 1)
                act.wait_ge(projected, 2 * k + 2)
                nc.scalar.activation(halves(sz), two(2), ACT.Silu).then_inc(activated, 1)
                act.wait_ge(convolved, 3 * k + 3)
                nc.scalar.activation(xc, v, ACT.Silu, bias=c.W(d + "_cb")).then_inc(activated, 1)
                act.wait_ge(low, k + 1)
                nc.scalar.activation(halves(dlow), two(4, DTR), ACT.Copy).then_inc(lowcopied, 1)
                act.wait_ge(dtproj, k + 1)
                nc.scalar.activation(halves(ea), two(0), ACT.Abs, bias=c.W(d + "_dtb")).then_inc(aready, 1)
                nc.scalar.activation(halves(eb), two(0), ACT.Relu, bias=c.W(d + "_dtb")).then_inc(soft, 1)
                act.wait_ge(aready, 3 * k + 1)
                nc.scalar.activation(ec, ea, ACT.Exp, scale=-1.0).then_inc(aready, 1)
                act.wait_ge(aready, 3 * k + 2)
                nc.scalar.activation(ed, ec, ACT.Ln, bias=1.0).then_inc(aready, 1)
                act.wait_ge(dtready, k + 1)
                for n in range(DS):
                    g = k * DS + n
                    if g >= 2:
                        act.wait_ge(state, g - 1)
                    nc.scalar.activation(dA[g % 2], dt, ACT.Exp, scale=c.An[:, k, n:n + 1]).then_inc(decay, 1)

        @block.vector
        def _(dve):
            link = linker(dve, chain)
            for k, d in enumerate("fb"):
                cw = c.W(d + "_cw")
                if k == 0:
                    dve.wait_ge(padded, 3)
                else:
                    dve.wait_ge(gated, 1)
                c.fetch.hook(dve, 6)
                dve.wait_ge(evacuated, k + 1)
                link(nc.vector.tensor_scalar(v, xin[:, DC - 1:DC - 1 + TW], cw[:, DC - 1:DC], None, ALU.mult))
                for j in range(DC - 1):
                    nc.vector.scalar_tensor_tensor(out=v, in0=xin[:, j:j + TW], scalar=cw[:, j:j + 1], in1=v,
                                                   op0=ALU.mult, op1=ALU.add).then_inc(convolved, 1)
                    dve.wait_ge(convolved, 3 * k + j + 1)
                dve.wait_ge(low, k + 1)
                if k:
                    dve.wait_ge(cready, DS)
                link(nc.vector.tensor_copy(halves(bcb[0:32, :]), two(6, 32)))
                link(nc.vector.tensor_tensor(halves(r1), two(6, 32), halves(bcb[0:32, :]), ALU.subtract))
                link(nc.vector.tensor_copy(mid, r1))
                link(nc.vector.tensor_tensor(r2, r1, mid, ALU.subtract))
                link(nc.vector.tensor_copy(bcb[32:64, :], mid))
                nc.vector.tensor_copy(bcb[64:96, :], r2).then_inc(split, 1)
                dve.wait_ge(aready, 3 * k + 3)
                dve.wait_ge(soft, k + 1)
                nc.vector.tensor_tensor(dt, eb, ed, ALU.add).then_inc(dtready, 1)
                dve.wait_ge(dtready, k + 1)
                link(nc.vector.tensor_tensor(dtx, dt, xc, ALU.mult))
                for n in range(DS):
                    g = k * DS + n
                    o = 4 * (g % 2)
                    dve.wait_ge(bready, g + 1)
                    nc.vector.tensor_tensor(halves(dBu[g % 2]), halves(dtx), two(o), ALU.mult).then_inc(inp, 1)
                    dve.wait_ge(decay, g + 1)
                    dve.wait_ge(inp, g + 1)
                    nc.vector.tensor_tensor_scan(hs[g % 2], dA[g % 2], dBu[g % 2], 0.0, ALU.mult, ALU.add).then_inc(state, 1)
                    dve.wait_ge(cready, g + 1)
                    dve.wait_ge(state, g + 1)
                    if g >= 2:
                        dve.wait_ge(summed, (g - 2) // DS * (DS + 1) + (g - 2) % DS + 2)
                    nc.vector.tensor_tensor(halves(hc[g % 2]), halves(hs[g % 2]), two(o + 2), ALU.mult).then_inc(outp, 1)
                    sums.append((c.fetch.eaten * HALF, c.fetch.limit()))
                    c.fetch.hook(dve, 1.7)
            dve.wait_ge(prod, 1)
            hf = c.h[:, :, :].rearrange("p t d -> p (t d)")
            link(nc.vector.tensor_tensor(hf, hf, c.ps[:, 0, 0:NT * D], ALU.add))
            link(nc.vector.tensor_tensor(c.h[:, :, :], c.h[:, :, :], c.y[:, :, :], ALU.add))

        @block.gpsimd
        def _(pool):
            c.clear(pool, c.last)
            nc.gpsimd.memset(xin[:, 0:DC - 1], 0.0).then_inc(padded, 1)
            for k in range(2):
                nc.gpsimd.memset(yd[k][:, TW:TP], 0.0).then_inc(padded, 1)
            for k, d in enumerate("fb"):
                c.fetch.issue(pool, sums[k * DS][0])
                pool.wait_ge(activated, 2 * k + 2)
                nc.gpsimd.tensor_scalar(yacc, xc, c.W(d + "_D"), None, ALU.mult).then_inc(summed, 1)
                for n in range(DS):
                    g = k * DS + n
                    c.fetch.issue(pool, sums[g][0])
                    pool.wait_ge(outp, g + 1)
                    pool.wait_ge(summed, k * (DS + 1) + n + 1)
                    nc.gpsimd.tensor_tensor(yacc, yacc, hc[g % 2], ALU.add).then_inc(summed, 1)
                    c.fetch.issue(pool, sums[g][1], most=2)
                pool.wait_ge(summed, (k + 1) * (DS + 1))
                nc.gpsimd.tensor_tensor(yd[k][:, 0:TW], yacc, sz, ALU.mult).then_inc(gated, 1)
            c.fetch.issue(pool, c.fetch.limit())
    c.last = "mamba"



def topk(c, b):
    nc = c.nc
    c.free()
    idx, wgt = (a[:, b % 2, :].rearrange("p (t h k) -> p t h k", h=PH, k=TOPK) for a in (c.idx_next, c.wgt_next))
    sim = [c.take(2 * PH * NK) for _ in range(2)]
    rest = c.take(2 * PH * NK).rearrange("p (s h k) -> p s h k", s=2, h=PH)
    v = c.take(2 * PH * TOPK).rearrange("p (s h k) -> p s h k", s=2, h=PH)
    vi = c.take(2 * PH * TOPK, dt=U32).rearrange("p (s h k) -> p s h k", s=2, h=PH)
    i0 = c.take(PH * TOPK).rearrange("p (h k) -> p h k", h=PH)
    i1 = c.take(PH * TOPK).rearrange("p (h k) -> p h k", h=PH)
    cand = c.take(PH * NCAND).rearrange("p (h k) -> p h k", h=PH)
    candi = c.take(PH * NCAND).rearrange("p (h k) -> p h k", h=PH)
    best = c.take(PH * TOPK).rearrange("p (h k) -> p h k", h=PH)
    pos = c.take(PH * TOPK, dt=U32).rearrange("p (h k) -> p h k", h=PH)
    posf = c.take(PH * TOPK).rearrange("p (h k) -> p h k", h=PH)
    hot = c.take(PH // 2 * TOPK * NCAND).rearrange("p (h k n) -> p h k n", h=PH // 2, k=TOPK)
    shifted = c.take(PH * TOPK).rearrange("p (h k) -> p h k", h=PH)
    ex = c.take(PH * TOPK).rearrange("p (h k) -> p h k", h=PH)
    z, rz = c.take(PH), c.take(PH)
    chain, scored, copied, taken, shift, expd = c.sems("topk", ["chain", "scored", "copied", "taken", "shift", "exp"])

    def largest(dve, link, lists):
        for src, _, top, _ in lists:
            last = nc.vector.max(out=top[:, 0:8], in_=src)
            c.fetch.hook(dve, 0.3)
        link(last)
        for src, left, top, _ in lists:
            last = nc.vector.match_replace(out=left, in_to_replace=top[:, 0:8], in_values=src, imm_value=-BIG)
            c.fetch.hook(dve, 0.3)
        link(last)
        for _, left, top, _ in lists:
            last = nc.vector.max(out=top[:, 8:16], in_=left)
            c.fetch.hook(dve, 0.3)
        link(last)
        for src, left, top, place in lists:
            nc.vector.max_index(out=place[:, 0:8], in_max=top[:, 0:8], in_values=src)
            last = nc.vector.max_index(out=place[:, 8:16], in_max=top[:, 8:16], in_values=left)
            c.fetch.hook(dve, 0.6)
        return last

    with nc.Block() as block:
        @block.tensor
        def _(pe):
            for i in range(NT):
                if i >= 2:
                    pe.wait_ge(copied, i - 1)
                for s in range(2):
                    last = pe.matmul(c.ps[:, i % 2 * 2 + s, :], c.yT[0:D, i * P:(i + 1) * P],
                                     c.fold[:, s, :, :].rearrange("p h k -> p (h k)"), start=True, stop=True)
                last.then_inc(scored, 1)

        @block.scalar
        def _(act):
            for i in range(NT):
                act.wait_ge(scored, i + 1)
                if i >= 2:
                    act.wait_ge(taken, i - 1)
                nc.scalar.activation(sim[i % 2].rearrange("p (s n) -> p s n", s=2),
                                     c.ps[:, i % 2 * 2:i % 2 * 2 + 2, :], ACT.Copy).then_inc(copied, 1)
                if i >= 1:
                    act.wait_ge(shift, i)
                    nc.scalar.activation(ex, shifted, ACT.Exp).then_inc(expd, 1)
            act.wait_ge(shift, NT)
            nc.scalar.activation(ex, shifted, ACT.Exp).then_inc(expd, 1)

        @block.vector
        def _(dve):
            link = linker(dve, chain)
            nc.vector.tensor_copy(c.hall[:, one(b), :], c.h[:, :, :].rearrange("p t d -> p (t d)").unsqueeze(1))
            for i in range(NT):
                dve.wait_ge(copied, i + 1)
                largest(dve, link, [(sim[i % 2][:, (s * PH + h) * NK:(s * PH + h + 1) * NK], rest[:, s, h, :],
                                     v[:, s, h, :], vi[:, s, h, :]) for s in range(2) for h in range(PH)]
                        ).then_inc(taken, 1)
                dve.wait_ge(taken, i + 1)
                nc.vector.tensor_copy(i0, vi[:, 0, :, :])
                link(nc.vector.scalar_tensor_tensor(out=i1, in0=vi[:, 1, :, :], scalar=float(NK),
                                                    in1=c.W("headoff").rearrange("p (h k) -> p h k", h=PH),
                                                    op0=ALU.mult, op1=ALU.add))
                for a, rows, length in GROUPS:
                    for dst, x0, x1 in ((cand, v[:, 0, :, :], v[:, 1, :, :]), (candi, i0, i1)):
                        o = dst[:, :, START[a]:START[a] + rows * length].rearrange("p h (a b) -> p h a b", b=length)
                        shape = [P, PH, rows, length]
                        last = nc.vector.tensor_tensor(o, bc(x0[:, :, a:a + rows], shape, 3),
                                                       bc(x1[:, :, 0:length], shape, 2), ALU.add)
                link(last)
                link(largest(dve, link, [(cand[:, h, :], rest[:, 0, h, 0:NCAND], best[:, h, :], pos[:, h, :])
                                         for h in range(PH)]))
                if i:
                    dve.wait_ge(expd, i)
                nc.vector.tensor_tensor(shifted, best, best[:, :, 0:1].to_broadcast([P, PH, TOPK]),
                                        ALU.subtract).then_inc(shift, 1)
                link(nc.vector.tensor_copy(posf, pos))
                iota = c.W("iota")[:, 0:NCAND]
                HH = PH // 2
                for q in range(2):
                    c.fetch.hook(dve, 5)
                    hh = slice(q * HH, (q + 1) * HH)
                    flat = hot.rearrange("p h k n -> p (h k) n")
                    pf = posf[:, hh, :].rearrange("p h k -> p (h k)")
                    link(nc.vector.tensor_tensor(flat, bc(pf, [P, HH * TOPK, NCAND], 2),
                                                 bc(iota, [P, HH * TOPK, NCAND], 1), ALU.is_equal))
                    link(nc.vector.tensor_tensor(hot, hot, bc(candi[:, hh, :], [P, HH, TOPK, NCAND], 2), ALU.mult))
                    link(nc.vector.reduce_sum(pf, flat, AX.X))
                link(nc.vector.tensor_copy(idx[:, i, :, :], posf))
                dve.wait_ge(expd, i + 1)
                link(nc.vector.reduce_sum(z, ex, AX.X))
                link(nc.vector.reciprocal(rz, z))
                link(nc.vector.tensor_tensor(wgt[:, i, :, :], ex, bc(rz, [P, PH, TOPK], 2), ALU.mult))

        @block.gpsimd
        def _(pool):
            c.clear(pool, c.last)
            c.fetch.issue(pool, c.fetch.limit())
    c.last = "topk"


def pk_project(c, kv, q, kT):
    nc = c.nc
    made, copied = c.sems("pkp", ["made", "copied"])
    n_units = 2 * (PH // 2) + 2 * (PH // 2)
    with nc.Block() as block:
        @block.tensor
        def _(pe):
            u = 0
            for hp in range(PH // 2):
                for s in range(2):
                    if u >= 4:
                        pe.wait_ge(copied, u - 3)
                    pe.matmul(c.ps[:, u % 4, 0:TP // 2], c.W("pk_wq")[:, hp * P:(hp + 1) * P],
                              c.yT[0:D, s * TP // 2:(s + 1) * TP // 2], start=True, stop=True).then_inc(made, 1)
                    u += 1
            for hp in range(PH // 2):
                for s in range(2):
                    pe.wait_ge(copied, u - 3)
                    for i in range(3 * s, 3 * s + 3):
                        last = pe.transpose(c.ps[:, u % 4, i % 3 * P:(i % 3 + 1) * P],
                                            kv[:, i, 0, 2 * hp * D:(2 * hp + 2) * D], c.W("ident"))
                    last.then_inc(made, 1)
                    u += 1

        @block.scalar
        def _(act):
            for u in range(n_units):
                act.wait_ge(made, u + 1)
                hp, s = u % 8 // 2, u % 2
                dst = (q[:, s * NT // 2:(s + 1) * NT // 2, hp, :] if u < 8 else
                       kT[:, hp, s * TP // 2:(s + 1) * TP // 2].rearrange("p (t n) -> p t n", n=P))
                nc.scalar.activation(dst, c.ps[:, u % 4, 0:TP // 2].rearrange("p (t n) -> p t n", n=P), ACT.Copy,
                                     scale=(float(D) ** -0.5 if u < 8 else 1.0)).then_inc(copied, 1)

        @block.vector
        def _(dve):
            nc.vector.tensor_copy(c.pv[:, :, :], c.kv[:, :, 1, :])

        @block.gpsimd
        def _(pool):
            c.clear(pool, c.last)
            c.fetch.issue(pool, c.fetch.limit())
    c.last = "pkp"



def attention(c, heads, span, q, k, v, dv, out, masks=None, rowscale=None, finish=None, pos=None):
    nc = c.nc
    at = c.at
    wide = max(min(span(j)[1] * P, T) - span(j)[0] * P for j in range(NT))
    wide = -(-wide // P) * P
    units = [(j, h) for j in range(NT) for h in range(heads)]
    probs = [c.take(wide) for _ in range(2)]
    turned = [c.take(4 * P) for _ in range(4)]
    nmax, nb, zs = c.take(len(units)), c.take(len(units)), c.take(len(units))
    rz = c.take(heads)
    sc = [c.take(wide) for _ in range(2)] if pos else None
    lin = [c.take(wide) for _ in range(2)] if pos else None
    per = P // dv
    sumw = heads // per * P
    lifted = c.take(sumw)
    chain, scored, biased, expd, tready, copy_a, copy_v, summed, normed, linear, lift, back = c.sems(
        "attention", ["chain", "scored", "biased", "exp", "turned", "copied_act", "copied_dve", "summed", "normed",
                      "linear", "lifted", "turned_back"])
    chunks = []
    for u, (j, h) in enumerate(units):
        t0, t1 = span(j)
        for t in range(t0, t1, 4):
            chunks.append((u, t, min(t + 4, t1)))
    of = [[n for n, ch in enumerate(chunks) if ch[0] == u] for u in range(len(units))]
    def cols(j):
        t0, t1 = span(j)
        return min(t1 * P, T) - t0 * P

    narrow = wide <= 512

    def sbank(u):
        return u % 2 if narrow else u % 2 * 2

    def S(u, w):
        b = sbank(u)
        return c.ps[:, b, 0:w] if narrow else c.ps[:, b:b + 2, :].rearrange("p b n -> p (b n)")[:, 0:w]

    def O(j):
        if sumw <= 512:
            return c.ps[:, 6 + j % 2, 0:sumw]
        assert narrow
        b = 2 if j % 2 == 0 else 6
        return c.ps[:, b:b + 2, :].rearrange("p b n -> p (b n)")[:, 0:sumw]

    def rows(t):
        return min(P, T - t * P)

    with nc.Block() as block:
        @block.tensor
        def _(pe):
            def scores(u):
                j, h = units[u]
                if u >= 2:
                    pe.wait_ge(expd, u - 1)
                t0 = span(j)[0]
                w = cols(j)
                ms = masks(j) if masks else []
                for a in range(0, w, 512):
                    b = min(a + 512, w)
                    here = [(m0, m1, m) for m0, m1, m in ms if a <= m0 < b]
                    last = pe.matmul(c.ps[:, sbank(u) + a // 512, 0:b - a], q(h, j), k(h, t0 * P + a, t0 * P + b),
                                     start=True, stop=True)
                    for n, (m0, m1, m) in enumerate(here):
                        m1 = min(m1, b)
                        last = pe.matmul(c.ps[:, sbank(u) + a // 512, m0 - a:m1 - a], c.identb[:, :], m[:, 0:m1 - m0],
                                         start=False, stop=True, skip_group_check=True)
                last.then_inc(scored, 1)

            def turn(n):
                u, a, b = chunks[n]
                pe.wait_ge(expd, u + 1)
                if n >= 2:
                    pe.wait_ge((copy_a, copy_v)[n % 2], n // 2)
                t0 = span(units[u][0])[0]
                for t in range(a, b):
                    last = pe.transpose(c.ps[0:rows(t), 4 + n % 2, (t - a) * P:(t - a + 1) * P],
                                        probs[u % 2][:, (t - t0) * P:(t - t0) * P + rows(t)], c.W("ident"))
                last.then_inc(tready, 1)

            def times_v(n):
                u, a, b = chunks[n]
                j, h = units[u]
                pe.wait_ge((copy_a, copy_v)[n % 2], n // 2 + 1)
                if h == 0 and a == span(j)[0] and j >= 2:
                    pe.wait_ge(normed, j - 1)
                t0, t1 = span(j)
                o = O(j)[h % per * dv:(h % per + 1) * dv, h // per * P:(h // per + 1) * P]
                for t in range(a, b):
                    last = pe.matmul(o, v(h, t), turned[n % 4][0:rows(t), (t - a) * P:(t - a + 1) * P],
                                     start=(t == t0), stop=(t == t1 - 1))
                last.then_inc(summed, 1)

            def turn_back(j):
                pe.wait_ge(lift, j + 1)
                for g in range(heads // per):
                    last = pe.transpose(O(j)[:, g * P:(g + 1) * P], lifted[:, g * P:(g + 1) * P], c.W("ident"))
                last.then_inc(back, 1)

            if not pos:
                scores(0)
            for u in range(len(units)):
                if not pos and u + 1 < len(units):
                    scores(u + 1)
                for n in of[u]:
                    turn(n)
                if u:
                    for n in of[u - 1]:
                        times_v(n)
                if units[u][1] == 2 and units[u][0]:
                    turn_back(units[u][0] - 1)
            for n in of[-1]:
                times_v(n)
            turn_back(NT - 1)

        def copy(eng, n):
            u, a, b = chunks[n]
            eng.wait_ge(tready, n + 1)
            if n >= 4:
                eng.wait_ge(summed, n - 3)
            parts = [(a, b, P)] if rows(b - 1) == P else [(a, b - 1, P), (b - 1, b, rows(b - 1))]
            ins = None
            for x, y, r in parts:
                if x == y:
                    continue
                dst, src = turned[n % 4][0:r, (x - a) * P:(y - a) * P], c.ps[0:r, 4 + n % 2, (x - a) * P:(y - a) * P]
                if n % 2 == 0:
                    ins = nc.scalar.activation(dst, src, ACT.Copy)
                else:
                    ins = nc.vector.tensor_copy(dst, src)
            ins.then_inc((copy_a, copy_v)[n % 2], 1)

        @block.scalar
        def _(act):
            def lift_sums(j):
                act.wait_ge(summed, of[(j + 1) * heads - 1][-1] + 1)
                if j:
                    act.wait_ge(back, j)
                nc.scalar.activation(lifted, O(j), ACT.Copy).then_inc(lift, 1)

            for u, (j, h) in enumerate(units):
                w = cols(j)
                if pos:
                    if u >= 2:
                        act.wait_ge(scored, u - 1)
                    nc.scalar.activation(lin[u % 2][:, 0:w], pos.dist(j), ACT.Identity, scale=pos.w0(h),
                                         bias=pos.b(h)).then_inc(linear, 1)
                act.wait_ge(biased, u + 1)
                if u >= 2:
                    act.wait_ge(tready, of[u - 2][-1] + 1)
                nc.scalar.activation(probs[u % 2][:, 0:w], sc[u % 2][:, 0:w] if pos else S(u, w), ACT.Exp,
                                     bias=nb[:, u:u + 1], scale=rowscale(h, j) if rowscale else 1.0,
                                     accum_out=zs[:, u:u + 1]).then_inc(expd, 1)
                if u:
                    for n in of[u - 1]:
                        if n % 2 == 0:
                            copy(act, n)
                if h == 1 and j:
                    lift_sums(j - 1)
            for n in of[-1]:
                if n % 2 == 0:
                    copy(act, n)
            lift_sums(NT - 1)

        @block.vector
        def _(dve):
            link = linker(dve, chain)

            def end_tile(j):
                dve.wait_ge(back, j + 1)
                z = zs[:, j * heads:(j + 1) * heads]
                link(nc.vector.reciprocal(rz, z))
                if finish:
                    finish(j, z, rz, O(j), link).then_inc(normed, 1)
                else:
                    nc.vector.tensor_tensor(out[:, j, :].rearrange("p (h d) -> p h d", h=heads),
                                            O(j).rearrange("p (h d) -> p h d", h=heads),
                                            bc(rz, [P, heads, dv], 2), ALU.mult).then_inc(normed, 1)

            for u, (j, h) in enumerate(units):
                w = cols(j)
                if pos:
                    dve.wait_ge(linear, u + 1)
                    if u >= 2:
                        dve.wait_ge(expd, u - 1)
                    nc.vector.scalar_tensor_tensor(out=sc[u % 2][:, 0:w], in0=pos.dist2(j), scalar=pos.w2(h),
                                                   in1=lin[u % 2][:, 0:w], op0=ALU.mult, op1=ALU.add).then_inc(scored, 1)
                dve.wait_ge(scored, u + 1)
                src = sc[u % 2][:, 0:w] if pos else S(u, w)
                if rowscale:
                    link(nc.vector.tensor_reduce(nmax[:, u:u + 1], src, AX.X, ALU.max, negate=True))
                    nc.vector.tensor_tensor(nb[:, u:u + 1], nmax[:, u:u + 1], rowscale(h, j), ALU.mult).then_inc(biased, 1)
                else:
                    nc.vector.tensor_reduce(nb[:, u:u + 1], src, AX.X, ALU.max, negate=True).then_inc(biased, 1)
                if u:
                    for n in of[u - 1]:
                        if n % 2:
                            copy(dve, n)
                    if h == 3 and j:
                        end_tile(j - 1)
                c.fetch.hook(dve, 0.4 + w / 250)
            for n in of[-1]:
                if n % 2:
                    copy(dve, n)
            end_tile(NT - 1)

        @block.gpsimd
        def _(pool):
            c.clear(pool, c.last)
            c.fetch.issue(pool, c.fetch.limit())
    c.last = "attention"
    c.free(at)


def project(c, src, weight, chunks, bias=None):
    nc = c.nc
    at = c.at
    width = src.shape[2] // chunks
    turned = [c.take(4 * P) for _ in range(2)]
    chain, tready, copied, done = c.sems("project", ["chain", "turned", "copied", "done"])
    groups = []
    for i in range(NT):
        for a in range(0, chunks, 4):
            groups.append((i, a, min(a + 4, chunks)))
    with nc.Block() as block:
        @block.tensor
        def _(pe):
            def product(n):
                i, a, b = groups[n]
                pe.wait_ge(copied, n + 1)
                for m in range(a, b):
                    last = pe.matmul(c.ps[:, 7, i * D:(i + 1) * D], turned[n % 2][0:width, (m - a) * P:(m - a + 1) * P],
                                     weight(m), start=(m == 0), stop=(m == chunks - 1))
                last.then_inc(done, 1)

            for n, (i, a, b) in enumerate(groups):
                if n >= 2:
                    pe.wait_ge(copied, n - 1)
                for m in range(a, b):
                    last = pe.transpose(c.ps[0:width, n % 2, (m - a) * P:(m - a + 1) * P],
                                        src[:, i, m * width:(m + 1) * width], c.W("ident"))
                last.then_inc(tready, 1)
                if n:
                    product(n - 1)
            product(len(groups) - 1)

        @block.scalar
        def _(act):
            for n, (i, a, b) in enumerate(groups):
                act.wait_ge(tready, n + 1)
                if n >= 2:
                    act.wait_ge(done, n - 1)
                nc.scalar.activation(turned[n % 2][0:width, 0:(b - a) * P], c.ps[0:width, n % 2, 0:(b - a) * P],
                                     ACT.Copy).then_inc(copied, 1)

        @block.vector
        def _(dve):
            link = linker(dve, chain)
            if bias is not None:
                link(nc.vector.tensor_tensor(c.h[:, :, :], c.h[:, :, :], bc(bias, [P, NT, D], 1), ALU.add))
            for _ in groups:
                c.fetch.hook(dve, 1.6)
            dve.wait_ge(done, len(groups))
            hf = c.h[:, :, :].rearrange("p t d -> p (t d)")
            nc.vector.tensor_tensor(hf, hf, c.ps[:, 7, 0:NT * D], ALU.add)

        @block.gpsimd
        def _(pool):
            c.clear(pool, c.last)
            c.fetch.issue(pool, c.fetch.limit())
    c.last = "project"
    c.free(at)



def ssm(c):
    nc = c.nc
    c.free()
    st = c.take(TP, D)
    made, ran, out, zero = c.sems("ssm", ["made", "ran", "out", "zero"])
    with nc.Block() as block:
        @block.tensor
        def _(pe):
            for s in range(2):
                last = pe.matmul(c.ps[0:D, s, 0:TW // 2], c.W("ssm_B"), c.yT[0:D, s * (TW // 2):(s + 1) * (TW // 2)],
                                 start=True, stop=True)
            last.then_inc(made, 1)
            pe.wait_ge(ran, 2)
            pe.wait_ge(zero, 1)
            for i in range(NT):
                last = pe.matmul(c.ps[:, 2, i * D:(i + 1) * D], st[:, i * P:(i + 1) * P], c.W("ssm_C"),
                                 start=True, stop=True)
            last.then_inc(out, 1)

        @block.vector
        def _(dve):
            dve.wait_ge(made, 1)
            a = c.W("ssm_A").to_broadcast([D, TW // 2])
            nc.vector.tensor_tensor_scan(st[:, 0:TW // 2], a, c.ps[0:D, 0, 0:TW // 2], c.W("ssm_h0"), ALU.mult,
                                         ALU.add).then_inc(ran, 1)
            dve.wait_ge(ran, 1)
            nc.vector.tensor_tensor_scan(st[:, TW // 2:TW], a, c.ps[0:D, 1, 0:TW // 2],
                                         st[:, TW // 2 - 1:TW // 2], ALU.mult, ALU.add).then_inc(ran, 1)
            dve.wait_ge(out, 1)
            hf = c.h[:, :, :].rearrange("p t d -> p (t d)")
            nc.vector.tensor_tensor(hf, hf, c.ps[:, 2, 0:NT * D], ALU.add)

        @block.gpsimd
        def _(pool):
            c.clear(pool, c.last)
            nc.gpsimd.memset(st[:, TW:TP], 0.0).then_inc(zero, 1)
            c.fetch.issue(pool, c.fetch.limit())
    c.last = "ssm"



def experts(c, m, kind, func, nf):
    nc = c.nc
    c.free()
    HB = TP // 2
    lg, ex, eq0, eq1, cw, t8 = (c.take(NT * E).rearrange("p (t e) -> p t e", e=E) for _ in range(6))
    top = c.take(NT * 8).rearrange("p (t e) -> p t e", e=8)
    topi = c.take(NT * 8, dt=U32).rearrange("p (t e) -> p t e", e=8)
    topf = c.take(NT * 8).rearrange("p (t e) -> p t e", e=8)
    s1, s2, s3, s4 = (c.take(NT) for _ in range(4))
    run = c.take(NT * E).rearrange("p (t e) -> p t e", e=E)
    hid = [c.take(TP) for _ in range(3)]
    acc = c.take(NT * D).rearrange("p (t d) -> p t d", d=D)
    tmp = c.take(NT * D).rearrange("p (t d) -> p t d", d=D)
    good = c.take(NT * D, dt=U32).rearrange("p (t d) -> p t d", d=D)
    lim = c.take(NT * D).rearrange("p (t d) -> p t d", d=D)
    chain, gated, h1, act_done, downed, yused, sh, exd, hot, counted = c.sems(
        m, ["chain", "gated", "h1", "act", "down", "y_used", "shifted", "exp", "hot", "counted"])
    full8, fullD = [P, NT, E], [P, NT, D]
    steps = [(e, f) for e in range(E) for f in range(nf)]
    F = nf * P
    with nc.Block() as block:
        @block.tensor
        def _(pe):
            for i in range(NT):
                last = pe.matmul(c.ps[:, 7, i * E:(i + 1) * E], c.yT[:, i * P:(i + 1) * P], c.W(m + "_g"),
                                 start=True, stop=True)
            last.then_inc(gated, 1)

            def down(n):
                e, f = steps[n]
                pe.wait_ge(act_done, n + 1)
                o = c.ps[:, 4 + e % 2, 0:NT * D]
                if f == 0:
                    if e >= 2:
                        pe.wait_ge(yused, e - 1)
                    b2 = c.W(m + "_b2")[:, e * D:(e + 1) * D]
                    pe.matmul(o.rearrange("p (t d) -> p t d", d=D), c.W("ones")[0:1, :], bc(b2, [1, NT, D], 1),
                              start=True, stop=True, skip_group_check=True)
                w2 = c.W(m + "_w2")[:, (f * E + e) * D:(f * E + e + 1) * D]
                for i in range(NT):
                    last = pe.matmul(o[:, i * D:(i + 1) * D], hid[n % 3][:, i * P:(i + 1) * P], w2, start=False,
                                     stop=True, skip_group_check=True)
                last.then_inc(downed, 1)

            for n, (e, f) in enumerate(steps):
                if n >= 2:
                    pe.wait_ge(act_done, n - 1)
                for s in range(2):
                    last = pe.matmul(c.ps[:, n % 2 * 2 + s, 0:HB],
                                     c.W(m + "_w1")[:, e * F + f * P:e * F + (f + 1) * P],
                                     c.yT[0:D, s * HB:(s + 1) * HB], start=True, stop=True)
                last.then_inc(h1, 1)
                if n == 1 and kind == "capacity":
                    pe.wait_ge(hot, 1)
                    flat = eq0.rearrange("p t e -> p (t e)")
                    pe.matmul(c.ps[:, 6, 0:NT * E], c.W("tri"), flat, start=True, stop=True)
                    pe.matmul(c.ps[:, 6, 64:64 + NT * E], c.W("ones"), flat, start=True, stop=True).then_inc(counted, 1)
                if n:
                    down(n - 1)
            down(len(steps) - 1)

        @block.scalar
        def _(act):
            act.wait_ge(sh, 1)
            if kind == "top2_logits":
                nc.scalar.activation(s2, s1, ACT.Exp).then_inc(exd, 1)
            else:
                nc.scalar.activation(ex, t8, ACT.Exp).then_inc(exd, 1)
            for n, (e, f) in enumerate(steps):
                act.wait_ge(h1, n + 1)
                if n >= 3:
                    act.wait_ge(downed, n - 2)
                b1 = c.W(m + "_b1")[:, f * E + e:f * E + e + 1]
                nc.scalar.activation(hid[n % 3].rearrange("p (s n) -> p s n", s=2),
                                     c.ps[:, n % 2 * 2:n % 2 * 2 + 2, 0:HB], func, bias=b1).then_inc(act_done, 1)

        @block.vector
        def _(dve):
            link = linker(dve, chain)
            dve.wait_ge(gated, 1)
            iota = bc(c.W("iota")[:, 0:E], full8, 1)
            link(nc.vector.tensor_copy(lg.rearrange("p t e -> p (t e)"), c.ps[:, 7, 0:NT * E]))
            if kind == "top2_logits":
                ranked = lg
            else:
                link(nc.vector.tensor_reduce(s1, lg, AX.X, ALU.max))
                nc.vector.tensor_tensor(t8, lg, bc(s1, full8, 2), ALU.subtract).then_inc(sh, 1)
                dve.wait_ge(exd, 1)
                link(nc.vector.reduce_sum(s2, ex, AX.X))
                link(nc.vector.reciprocal(s3, s2))
                link(nc.vector.tensor_tensor(lg, ex, bc(s3, full8, 2), ALU.mult))
                ranked = lg
            for i in range(NT):
                last = nc.vector.max(out=top[:, i, :], in_=ranked[:, i, :])
            link(last)
            for i in range(NT):
                last = nc.vector.max_index(out=topi[:, i, :], in_max=top[:, i, :], in_values=ranked[:, i, :])
            link(last)
            link(nc.vector.tensor_copy(topf, topi))
            link(nc.vector.tensor_tensor(eq0, iota, bc(topf[:, :, 0], full8, 2), ALU.is_equal))
            if kind == "capacity":
                nc.vector.tensor_tensor(eq0, eq0, bc(c.W("valid"), full8, 2), ALU.mult).then_inc(hot, 1)
                dve.wait_ge(counted, 1)
                for i in range(NT):
                    before = c.carry[:, :] if i == 0 else run[:, i - 1, :]
                    link(nc.vector.tensor_tensor(run[:, i, :], before, c.ps[:, 6, 64 + i * E:64 + (i + 1) * E], ALU.add))
                link(nc.vector.tensor_copy(t8, c.ps[:, 6, 0:NT * E].rearrange("p (t e) -> p t e", e=E)))
                nc.vector.tensor_tensor(t8[:, 0, :], t8[:, 0, :], c.carry[:, :], ALU.add)
                link(nc.vector.tensor_tensor(t8[:, 1:, :], t8[:, 1:, :], run[:, 0:NT - 1, :], ALU.add))
                nc.vector.tensor_copy(c.carry[:, :], run[:, NT - 1, :])
                link(nc.vector.tensor_tensor(t8, t8, eq0, ALU.mult))
                link(nc.vector.reduce_sum(s1, t8, AX.X))
                link(nc.vector.tensor_scalar(s2, s1, float(CAP), None, ALU.is_le))
                link(nc.vector.tensor_tensor(s3, s2, top[:, :, 0], ALU.mult))
                link(nc.vector.tensor_tensor(cw, eq0, bc(s3, full8, 2), ALU.mult))
            else:
                link(nc.vector.tensor_tensor(eq1, iota, bc(topf[:, :, 1], full8, 2), ALU.is_equal))
                if kind == "top2_logits":
                    nc.vector.tensor_tensor(s1, top[:, :, 1], top[:, :, 0], ALU.subtract).then_inc(sh, 1)
                    dve.wait_ge(exd, 1)
                    link(nc.vector.tensor_scalar(s3, s2, 1.0, None, ALU.add))
                    link(nc.vector.reciprocal(s4, s3))
                    link(nc.vector.tensor_tensor(s3, s2, s4, ALU.mult))
                    w0, w1 = s4, s3
                else:
                    w0, w1 = top[:, :, 0], top[:, :, 1]
                link(nc.vector.tensor_tensor(eq0, eq0, bc(w0, full8, 2), ALU.mult))
                link(nc.vector.tensor_tensor(eq1, eq1, bc(w1, full8, 2), ALU.mult))
                link(nc.vector.tensor_tensor(cw, eq0, eq1, ALU.add))
            for e in range(E):
                dve.wait_ge(downed, nf * (e + 1))
                ye = c.ps[:, 4 + e % 2, 0:NT * D].rearrange("p (t d) -> p t d", d=D)
                dst = tmp if e else acc
                nc.vector.tensor_tensor(dst, ye, bc(cw[:, :, e], fullD, 2), ALU.mult).then_inc(yused, 1)
                dve.wait_ge(yused, e + 1)
                if e:
                    link(nc.vector.tensor_tensor(acc, acc, tmp, ALU.add))
                c.fetch.hook(dve, 6.5 * nf)
            if kind == "capacity":
                nc.vector.memset(lim, 1.0e4)
                link(nc.vector.memset(tmp, 0.0))
                link(nc.vector.tensor_tensor(good, acc, acc, ALU.is_equal))
                link(nc.vector.copy_predicated(tmp, good, acc))
                link(nc.vector.tensor_scalar(good, acc, FMAX, None, ALU.is_gt))
                link(nc.vector.copy_predicated(tmp, good, lim))
                nc.vector.memset(lim, -1.0e4)
                link(nc.vector.tensor_scalar(good, acc, -FMAX, None, ALU.is_lt))
                link(nc.vector.copy_predicated(tmp, good, lim))
                acc_ = tmp
            else:
                acc_ = acc
            nc.vector.tensor_tensor(c.h[:, :, :], c.h[:, :, :], acc_, ALU.add)

        @block.gpsimd
        def _(pool):
            c.clear(pool, c.last)
            c.fetch.issue(pool, c.fetch.limit())
    c.last = m



def rotary(c, q, kT, v, rs):
    nc = c.nc
    at = c.at
    HB = TP // 2
    tmp, sq = ([c.take(HB).rearrange("p (t n) -> p t n", n=P) for _ in range(2)] for _ in range(2))
    ssq = c.take(NT * QH)
    rk = c.take(TP)
    chain, made, prod, rot, sqd, vready, normq, root, summed = c.sems(
        "rotary", ["chain", "made", "products", "rotated", "squared", "v", "square_sums", "root", "means"])
    units = [(hp, s) for hp in range(QH // 2 + 1) for s in range(2)]
    NQ = QH // 2

    def halves(v):
        return v.rearrange("p (t n) -> p t n", n=P)

    def dst(hp, s):
        t = slice(s * NT // 2, (s + 1) * NT // 2)
        return q[:, t, hp, :] if hp < NQ else halves(kT)[:, t, :]

    with nc.Block() as block:
        @block.tensor
        def _(pe):
            for i in range(NT):
                last = pe.matmul(c.ps[:, 7, i * D:(i + 1) * D], c.yT[0:D, i * P:(i + 1) * P], c.W("wa_v"),
                                 start=True, stop=True)
            last.then_inc(vready, 1)

            def squares(u):
                hp, s = units[u]
                pe.wait_ge(sqd, u + 1)
                if hp < NQ:
                    for i in range(3):
                        t = 3 * s + i
                        last = pe.matmul(c.ps[:, 6, t * QH + 2 * hp:t * QH + 2 * hp + 2], sq[u % 2][:, i, :],
                                         c.W("blockones")[:, 0:P:D], start=True, stop=True)
                else:
                    last = pe.matmul(c.ps[:, s, 0:HB], c.W("blockones"), sq[u % 2].rearrange("p t n -> p (t n)"), start=True, stop=True)
                last.then_inc(normq, 1)

            for u, (hp, s) in enumerate(units):
                if u >= 3:
                    pe.wait_ge(prod, 2 * (u - 2))
                wq = c.W("wa_q")[:, hp * P:(hp + 1) * P] if hp < NQ else c.W("wa_k")
                ws = c.W("wa_qs")[:, hp * P:(hp + 1) * P] if hp < NQ else c.W("wa_ks")
                x = c.yT[0:D, s * HB:(s + 1) * HB]
                pe.matmul(c.ps[:, 2 * (u % 3), 0:HB], wq, x, start=True, stop=True)
                pe.matmul(c.ps[:, 2 * (u % 3) + 1, 0:HB], ws, x, start=True, stop=True).then_inc(made, 1)
                if u >= 2 and units[u - 2][0] < NQ:
                    squares(u - 2)
            pe.wait_ge(prod, 2 * len(units))
            for u in range(len(units) - 2, len(units)):
                squares(u)

        @block.scalar
        def _(act):
            act.wait_ge(vready, 1)
            nc.scalar.activation(v.rearrange("p t d -> p (t d)"), c.ps[:, 7, 0:NT * D], ACT.Copy)
            for u, (hp, s) in enumerate(units):
                act.wait_ge(rot, u + 1)
                if u >= 2:
                    act.wait_ge(normq, u - 1)
                nc.scalar.activation(sq[u % 2], dst(hp, s), ACT.Square).then_inc(sqd, 1)
            act.wait_ge(summed, 1)
            nc.scalar.activation(rs, ssq, ACT.Sqrt).then_inc(root, 1)
            act.wait_ge(summed, 2)
            nc.scalar.activation(rk, rk, ACT.Sqrt).then_inc(root, 1)

        @block.vector
        def _(dve):
            link = linker(dve, chain)
            for u, (hp, s) in enumerate(units):
                dve.wait_ge(made, u + 1)
                nc.vector.tensor_tensor(dst(hp, s), halves(c.ps[:, 2 * (u % 3), 0:HB]),
                                        halves(c.W("cos")[:, s * HB:(s + 1) * HB]), ALU.mult).then_inc(prod, 1)
                nc.vector.tensor_tensor(tmp[u % 2], halves(c.ps[:, 2 * (u % 3) + 1, 0:HB]),
                                        halves(c.W("sin")[:, s * HB:(s + 1) * HB]), ALU.mult).then_inc(prod, 1)
                dve.wait_ge(prod, 2 * u + 2)
                nc.vector.tensor_tensor(dst(hp, s), dst(hp, s), tmp[u % 2], ALU.add).then_inc(rot, 1)
                c.fetch.hook(dve, 4.0)
            dve.wait_ge(normq, len(units))
            nc.vector.tensor_scalar(ssq, c.ps[:, 6, 0:NT * QH], 1.0 / D, RMS_EPS, ALU.mult, ALU.add).then_inc(summed, 1)
            nc.vector.tensor_scalar(rk.rearrange("p (s n) -> p s n", s=2), c.ps[:, 0:2, 0:HB], 1.0 / D, RMS_EPS,
                                    ALU.mult, ALU.add).then_inc(summed, 1)
            dve.wait_ge(root, 2)
            link(nc.vector.reciprocal(rs, rs))
            link(nc.vector.reciprocal(rk, rk))
            link(nc.vector.tensor_scalar(rs, rs, float(D) ** -0.5, None, ALU.mult))
            link(nc.vector.scalar_tensor_tensor(out=kT, in0=kT, scalar=c.knw[:, 0:1], in1=rk, op0=ALU.mult, op1=ALU.mult))

        @block.gpsimd
        def _(pool):
            c.clear(pool, c.last)
            c.fetch.issue(pool, c.fetch.limit())
            c.fetch.issue(pool, c.fetch.limit())
    c.last = "rotary"
    c.free(at)



def gated_value(c, b):
    nc = c.nc
    (made,) = c.sems("gv", ["made"])
    with nc.Block() as block:
        @block.tensor
        def _(pe):
            for i in range(NT):
                last = pe.matmul(c.ps[:, 0, i * D:(i + 1) * D], c.yT[0:D, i * P:(i + 1) * P], c.W("ga_v"),
                                 start=True, stop=True)
            last.then_inc(made, 1)

        @block.vector
        def _(dve):
            nc.vector.tensor_copy(c.hall[:, one(b), :], c.h[:, :, :].rearrange("p t d -> p (t d)").unsqueeze(1))
            dve.wait_ge(made, 1)
            nc.vector.tensor_copy(c.vall[:, :, :, one(b), :].rearrange("p t h b d -> p (t h) (b d)"),
                                  c.ps[:, 0, 0:NT * D].rearrange("p (n d) -> p n d", d=GD))

        @block.gpsimd
        def _(pool):
            c.clear(pool, c.last)
            c.fetch.issue(pool, c.fetch.limit())
    c.last = "gv"


class Distances:

    def __init__(self, c, dist, dist2, bias):
        self.c, self.t, self.t2, self.bias = c, dist, dist2, bias

    def dist(self, j):
        return self.t[:, DOFF - j * P:DOFF - j * P + T]

    def dist2(self, j):
        return self.t2[:, DOFF - j * P:DOFF - j * P + T]

    def w0(self, h):
        return self.c.W("ga_wpos")[:, 3 * h:3 * h + 1]

    def w2(self, h):
        return self.c.W("ga_wpos")[:, 3 * h + 2:3 * h + 3]

    def b(self, h):
        return self.bias[:, h:h + 1]


def positional(c, dist):
    nc = c.nc
    c.free()
    t, t2, bias, a = c.take(DCOLS), c.take(DCOLS), c.take(GH), c.take(GH)
    loaded, chain = c.sems("dist", ["loaded", "chain"])
    with nc.Block() as block:
        @block.sync
        def _(sp):
            sp.dma_start(t, dist).then_inc(loaded, 16)

        @block.vector
        def _(dve):
            link = linker(dve, chain)
            dve.wait_ge(loaded, 16)
            link(nc.vector.tensor_tensor(t2, t, t, ALU.mult))
            w = c.W("ga_wpos").rearrange("p (h k) -> p h k", k=3)
            link(nc.vector.scalar_tensor_tensor(out=bias, in0=w[:, :, 1], scalar=0.0, in1=c.W("ga_bpos"),
                                                op0=ALU.mult, op1=ALU.add))

        @block.gpsimd
        def _(pool):
            c.clear(pool, c.last)
            c.fetch.issue(pool, c.fetch.limit())
    c.last = "dist"

    def finish(j, z, rz, o, link):
        link(nc.vector.tensor_tensor(a, rz, c.sg[:, :], ALU.mult))
        link(nc.vector.tensor_tensor(c.poss[:, j, :], a, z, ALU.mult))
        shape = [P, GH, B, GD]
        return nc.vector.tensor_tensor(c.poso[:, :, j, :].rearrange("p b (h d) -> p h b d", h=GH),
                                       o.rearrange("p (h b d) -> p h b d", h=GH, b=B),
                                       a.unsqueeze(2).unsqueeze(3).to_broadcast(shape), ALU.mult)

    attention(c, GH, lambda j: (0, NT), None, None,
              lambda h, t: c.vall[0:min(P, T - t * P), t, h, :, :].rearrange("p b d -> p (b d)"), B * GD, None,
              finish=finish, pos=Distances(c, t, t2, bias))


def gated_load(c, b, pcur, v, also_clear):
    nc = c.nc
    with nc.Block() as block:
        @block.vector
        def _(dve):
            nc.vector.tensor_copy(c.h[:, :, :].rearrange("p t d -> p (t d)").unsqueeze(1), c.hall[:, one(b), :])
            nc.vector.tensor_copy(pcur.rearrange("p t d -> p (t d)"),
                                  c.poso[:, one(b), :, :].rearrange("p b t d -> p (b t d)"))
            nc.vector.memset(v, 0.0)

        @block.gpsimd
        def _(pool):
            c.clear(pool, c.last, *also_clear)
            c.fetch.issue(pool, c.fetch.limit())
    c.last = None


def gated_project(c, q, k, v):
    nc = c.nc
    made, copied = c.sems("gp", ["made", "copied"])
    HB = TP // 2
    with nc.Block() as block:
        @block.tensor
        def _(pe):
            for u in range(8):
                g, s = u // 2 % 2, u % 2
                if u >= 4:
                    pe.wait_ge(copied, u - 3)
                pe.matmul(c.ps[:, u % 4, 0:HB], c.W("ga_q" if u < 4 else "ga_k")[:, g * P:(g + 1) * P],
                          c.yT[0:D, s * HB:(s + 1) * HB], start=True, stop=True).then_inc(made, 1)
            for i in range(NT):
                last = pe.matmul(c.ps[:, 4, i * D:(i + 1) * D], c.yT[0:D, i * P:(i + 1) * P], c.W("ga_v"),
                                 start=True, stop=True)
            last.then_inc(made, 1)

        @block.scalar
        def _(act):
            for u in range(8):
                g, s = u // 2 % 2, u % 2
                act.wait_ge(made, u + 1)
                nc.scalar.activation((q if u < 4 else k)[:, g, s * HB:(s + 1) * HB], c.ps[:, u % 4, 0:HB], ACT.Copy,
                                     scale=(float(GD) ** -0.5 if u < 4 else 1.0)).then_inc(copied, 1)
            act.wait_ge(made, 9)
            nc.scalar.activation(v.rearrange("p t (h r) -> p (t h) r", r=32)[:, :, 0:GD],
                                 c.ps[:, 4, 0:NT * D].rearrange("p (n d) -> p n d", d=GD), ACT.Copy)

        @block.gpsimd
        def _(pool):
            c.clear(pool, c.last)
            c.fetch.issue(pool, c.fetch.limit())
    c.last = "gp"


def store(c, out, b):
    nc = c.nc
    (stored,) = c.sems("store", ["stored"])
    full = (NT - 1) * P
    with nc.Block() as block:
        @block.sync
        def _(sp):
            o = out[one(b), 0:full, :].rearrange("b (t p) d -> p (b t) d", p=P)
            sp.dma_start(o, c.h[:, 0:NT - 1, :]).then_inc(stored, 16)
            sp.dma_start(out[one(b), full:T, :].rearrange("b p d -> (b p) d"), c.h[0:TAIL, NT - 1, :]).then_inc(stored, 16)
            sp.wait_ge(stored, 32)

        @block.gpsimd
        def _(pool):
            c.clear(pool, c.last)
            c.fetch.issue(pool, c.fetch.limit())
    c.last = "store"



def swap(c, rows=None, load=None):
    nc = c.nc
    with nc.Block() as block:
        @block.vector
        def _(dve):
            if load is not None:
                nc.vector.tensor_copy(c.h[:, :, :].rearrange("p t d -> p (t d)").unsqueeze(1), c.hall[:, one(load), :])
            if rows is not None:
                nc.vector.tensor_copy(c.idx[:, :].unsqueeze(1), c.idx_next[:, one(rows), :])
                nc.vector.tensor_copy(c.wgt[:, :].unsqueeze(1), c.wgt_next[:, one(rows), :])

        @block.gpsimd
        def _(pool):
            c.clear(pool, c.last)
    c.last = None


def front(c, x, b):
    conv(c, x, b)
    norm(c, c.h[:, :, :])
    mamba(c)
    norm(c, c.h[:, :, :])
    topk(c, b)


def back(c, b, fetch=None):
    half = lambda h: slice(h % 2 * D, h % 2 * D + D)
    def shared(heads):
        q = c.take(heads * NT * D).rearrange("p (t h n) -> p t h n", t=NT, n=P)
        return q, q.rearrange("p t h n -> p t (h n)")

    norm(c, c.h[:, :, :])
    c.free()
    q, o = shared(PH)
    k = c.take(PH // 2 * TP).rearrange("p (h n) -> p h n", n=TP)
    pk_project(c, c.kv, q, k)
    if fetch:
        fetch()
    attention(c, PH, lambda j: (0, j + 1),
              lambda h, j: q[half(h), j, h // 2, :],
              lambda h, lo, hi: k[half(h), h // 2, lo:hi],
              lambda h, t: c.pv[0:min(P, T - t * P), t, h * D:(h + 1) * D], D, o,
              masks=lambda j: [(j * P, (j + 1) * P, c.masksb[:, P:2 * P])])
    project(c, o, lambda m: c.W("pk_wo")[:, m * D:(m + 1) * D], PH * D // P)

    norm(c, c.h[:, :, :])
    ssm(c)
    norm(c, c.h[:, :, :])
    norm(c, c.y[:, :, :], affine=(c.W("gamma"), c.W("beta")), stage="ln2")
    experts(c, "m1", "top2_logits", ACT.Gelu, 1)

    norm(c, c.h[:, :, :])
    c.free()
    wq, wo = shared(QH)
    wk = c.take(TP)
    wv = c.take(NT * D).rearrange("p (t d) -> p t d", d=D)
    rs = c.take(NT * QH)
    rotary(c, wq, wk, wv, rs)
    attention(c, QH, lambda j: (max(j - 1, 0), j + 1),
              lambda h, j: wq[half(h), j, h // 2, :],
              lambda h, lo, hi: wk[half(h), lo:hi],
              lambda h, t: wv[0:min(P, T - t * P), t, :], D, wo,
              masks=lambda j: [(0, 2 * P, c.masksb[:, 0:2 * P])] if j else [(0, P, c.masksb[:, P:2 * P])],
              rowscale=lambda h, j: rs[:, j * QH + h:j * QH + h + 1])
    project(c, wo, lambda m: c.W("wa_o")[:, m * D:(m + 1) * D], QH * D // P)
    norm(c, c.h[:, :, :])
    experts(c, "m2", "capacity", ACT.Relu, 2)
    norm(c, c.h[:, :, :])
    gated_value(c, b)


def audio_tower(nc, x, weights, raw, dist, table, out, stop=99, dump=None):
    c = Core(nc)
    setup(c, weights, raw)
    gather = lambda every: c.fetch.start(table, every)
    front(c, x, 0)
    swap(c, rows=0)
    gather(7.7)
    front(c, x, 1)
    front(c, x, 2)
    c.fetch.finish()
    swap(c, rows=1, load=0)
    back(c, 0, fetch=lambda: gather(8.6))
    front(c, x, 3)
    c.fetch.finish()
    with nc.Fori(2, B) as b:
        swap(c, rows=b - 2, load=b - 1)
        back(c, b - 1, fetch=lambda: gather(6.6))
        c.fetch.finish()
    swap(c, load=B - 1)
    back(c, B - 1)
    positional(c, dist)
    with nc.Fori(0, B) as b:
        c.free()
        q = c.take(2 * TP).rearrange("p (g n) -> p g n", g=2)
        k = c.take(2 * TP).rearrange("p (g n) -> p g n", g=2)
        v = c.take(NT * GH * 32).rearrange("p (t n) -> p t n", t=NT)
        o = c.take(NT * D).rearrange("p (t d) -> p t d", d=D)
        pcur = c.take(NT * D).rearrange("p (t d) -> p t d", d=D)
        part, wsum, rsum = c.take(GH), c.take(GH), c.take(GH)
        at = c.at
        c.sems("store", ["stored"])
        gated_load(c, b, pcur, v, ("store",))
        norm(c, c.h[:, :, :])
        gated_project(c, q, k, v)

        def finish(j, z, rz, sums, link):
            shape = [P, GH, GD]
            oj = o[:, j, :].rearrange("p (h d) -> p h d", h=GH)
            link(nc.vector.tensor_tensor(part, rz, c.omg[:, :], ALU.mult))
            link(nc.vector.tensor_tensor(wsum, part, z, ALU.mult))
            link(nc.vector.tensor_tensor(wsum, wsum, c.poss[:, j, :], ALU.add))
            link(nc.vector.reciprocal(rsum, wsum))
            link(nc.vector.tensor_tensor(oj, sums.rearrange("p (h r) -> p h r", h=GH)[:, :, 0:GD], bc(part, shape, 2), ALU.mult))
            link(nc.vector.tensor_tensor(o[:, j, :], o[:, j, :], pcur[:, j, :], ALU.add))
            return nc.vector.tensor_tensor(oj, oj, bc(rsum, shape, 2), ALU.mult)

        rows = lambda h: slice(h % 4 * 32, h % 4 * 32 + GD)
        attention(c, GH, lambda j: (0, NT),
                  lambda h, j: q[rows(h), h // 4, j * P:(j + 1) * P],
                  lambda h, lo, hi: k[rows(h), h // 4, lo:hi],
                  lambda h, t: v[0:min(P, T - t * P), t, h * 32:(h + 1) * 32], 32, o, finish=finish)
        project(c, o, lambda m: c.W("ga_o"), 1, bias=c.W("ga_ob"))
        norm(c, c.h[:, :, :])
        experts(c, "m3", "top2_probs", ACT.Gelu, 1)
        store(c, out, b)



def shape_constants():
    p = np.arange(P)
    big = np.float32(-1e30)
    q, k = p[:, None], p[None, :]
    freqs = np.float32(10000.0) ** (np.float32(-2.0) * np.arange(D // 2, dtype=np.float32) / np.float32(D))
    theta = np.arange(TP, dtype=np.float32)[None, :] * freqs.astype(np.float32)[:, None]
    cos, sin = np.cos(theta), np.sin(theta)
    sgn = np.stack([-sin, sin], axis=1).reshape(D, TP)
    valid = np.ones((P, NT), np.float32)
    valid[TAIL:, NT - 1] = 0
    bsel = np.concatenate([np.eye(32, dtype=np.float32)] * 3)
    return {
        "ident": np.eye(P), "cos": np.tile(np.repeat(cos, 2, axis=0), (2, 1)), "sin": np.tile(sgn, (2, 1)),
        "masks": np.concatenate([np.where(k < q, big, 0), np.where(k > q, big, 0)], axis=1),
        "blockones": (q // D == k // D), "ones": np.ones((P, P)), "tri": (q <= k),
        "iota": np.broadcast_to(np.arange(64), (P, 64)),
        "headoff": np.broadcast_to(np.repeat(np.arange(PH) * NKV, TOPK), (P, PH * TOPK)),
        "valid": valid, "bsel": bsel,
    }


def packed(layout, parts):
    place, total = columns(layout)
    a = np.zeros((P, total), np.float32)
    for name, (rows, at, cols) in place.items():
        a[0:rows, at:at + cols] = np.asarray(parts[name], np.float32).reshape(rows, cols)
    return a


def lay_out(n):
    w = shape_constants()
    col = lambda a: np.asarray(a).reshape(-1, 1)
    wide = lambda a: np.broadcast_to(np.asarray(a).reshape(1, -1), (P, np.asarray(a).size))
    for d in "fb":
        g = lambda s: np.asarray(n[f"L0_attn_{d}_{s}"])
        in_w, out_w = g("in_w"), g("out_w")
        if d == "b":
            in_w, out_w = in_w[:, ::-1], out_w[::-1, :]
        w |= {d + "_in": in_w.T, d + "_cw": g("conv_w"), d + "_cb": col(g("conv_b")), d + "_xp": g("xproj_w").T,
              d + "_dtw": g("dt_w").T, d + "_dtb": col(g("dt_b")), d + "_alog": g("A_log"), d + "_D": col(g("D")),
              d + "_out": out_w.T}
    rows128 = lambda a: a.reshape(-1, P, a.shape[1]).transpose(1, 0, 2).reshape(P, -1)
    w |= {"pk_wq": n["L0_ffn_Wq"], "pk_wo": rows128(np.asarray(n["L0_ffn_Wo"]))}
    w |= {"ssm_A": col(n["L1_attn_A"]), "ssm_h0": col(n["L1_attn_h0"]), "ssm_B": n["L1_attn_B"], "ssm_C": n["L1_attn_C"]}
    w |= {"gamma": wide(n["L1_ffn_gamma"]), "beta": wide(n["L1_ffn_beta"])}
    for m, pre, names in (("m1", "L1_ffn_", ("Wr", "br", "W1", "b1", "W2", "b2")),
                          ("m2", "L2_ffn_", ("gate_w", "gate_b", "w1", "b1", "w2", "b2")),
                          ("m3", "L3_ffn_", ("gate_w", "gate_b", "W1", "b1", "W2", "b2"))):
        gw, gb, w1, b1, w2, b2 = (np.asarray(n[pre + s]) for s in names)
        f = w1.shape[2]
        w |= {m + "_g": np.concatenate([gw, gb[None]]), m + "_w1": w1.transpose(1, 0, 2),
              m + "_b1": b1.reshape(E, f // P, P).transpose(2, 1, 0),
              m + "_w2": w2.reshape(E, f // P, P, D).transpose(2, 1, 0, 3), m + "_b2": b2.reshape(1, -1)}
    wq, wkv, wo = (np.asarray(n["L2_attn_" + s]) for s in ("wq", "wkv", "wo"))
    swap = lambda a: a.reshape(-1, 2, D)[:, ::-1].reshape(-1, D)
    twice = lambda a: np.concatenate([a, a])
    wk, wv = wkv[:D], wkv[D:]
    w |= {"wa_q": wq.T, "wa_qs": swap(wq).T, "wa_k": twice(wk).T, "wa_ks": twice(swap(wk)).T, "wa_v": wv.T,
          "wa_qn": col(twice(np.asarray(n["L2_attn_q_norm_w"]))), "wa_kn": col(twice(np.asarray(n["L2_attn_k_norm_w"]))),
          "wa_o": rows128(wo.T)}
    wqk = np.asarray(n["L3_attn_Wqk"])

    def spread(a):
        o = np.zeros((GH, 32, D), np.float32)
        o[:, :GD] = a.reshape(GH, GD, D)
        return o.reshape(2 * P, D).T
    w |= {"ga_q": spread(wqk[:D]), "ga_k": spread(wqk[D:]), "ga_v": np.asarray(n["L3_attn_Wv"]).T,
          "ga_wpos": wide(n["L3_attn_Wpos"]), "ga_bpos": wide(n["L3_attn_bpos"]), "ga_g": wide(n["L3_attn_gating"]),
          "ga_o": np.asarray(n["L3_attn_Wproj"]).T, "ga_ob": wide(n["L3_attn_bproj"])}
    taps = lambda a: np.asarray(a).reshape(D, D, TAPS // 2, 2).transpose(3, 1, 2, 0)
    ph = np.asarray(n["L0_tok_phases"]).reshape(TAPS // 2, 2)
    pq = np.asarray(n["L0_ffn_Wq_pk"]).reshape(D, 2 * PH, DK).transpose(2, 1, 0)
    pk = np.asarray(n["L0_ffn_pk_keys"]).transpose(3, 0, 2, 1)
    raw = {"cv_r": taps(n["L0_tok_w_real"]), "cv_i": taps(n["L0_tok_w_imag"]), "cv_ph": np.repeat(ph.T, D, axis=0),
           "pk_q": pq, "pk_k": pk}
    x = np.asarray(n["x"])
    xp = np.zeros((B, 2, D, XC - 1), np.float32)
    xp[:, 0, :, :S_IN] = x.transpose(0, 2, 1)
    xp[:, 1, :, :S_IN - 1] = x.transpose(0, 2, 1)[:, :, 1:]
    dist = (np.arange(DCOLS)[None, :] - DOFF - np.arange(P)[:, None]).astype(np.float32)
    table = np.concatenate([np.asarray(n["L0_ffn_keys_table"]), np.asarray(n["L0_ffn_values_table"])], axis=1)
    return {"x": xp.reshape(B * P, XC - 1), "weights": packed(weight_layout(), w), "raw": packed(setup_layout(), raw),
            "dist": dist, "table": table}


def kernel(**inputs):
    import concourse.bacc as bacc
    from concourse.bass_utils import run_bass_kernel_spmd

    nc = bacc.Bacc("TRN2", target_bir_lowering=False, num_devices=1)
    arrays = {f"in_{k}_dram": np.ascontiguousarray(a) for k, a in lay_out(inputs).items()}
    args = [nc.dram_tensor(k, a.shape, mybir.dt.from_np(a.dtype), kind="ExternalInput").ap() for k, a in arrays.items()]
    out = nc.dram_tensor("out_dram", (B, T, D), F32, kind="ExternalOutput").ap()
    audio_tower(nc, *args, out)
    r = run_bass_kernel_spmd(nc, [arrays], core_ids=[0])
    return r.results[0]["out_dram"]
```
